# Optimizing a Trainium2 kernel written in Bass

```python
import numpy as np
import jax
import jax.numpy as jnp

def _softmax(x, axis=-1):
    return jax.nn.softmax(x, axis=axis)

def _gelu(x):
    return jax.nn.gelu(x, approximate=True)

def _silu(x):
    return jax.nn.silu(x)

def _sigmoid(x):
    return jax.nn.sigmoid(x)

def _layernorm(x, axis=-1, eps=1e-05):
    m = jnp.mean(x, axis=axis, keepdims=True)
    v = jnp.var(x, axis=axis, keepdims=True)
    return (x - m) / jnp.sqrt(v + eps)

def _scatter_add(tgt, idx, src, axis=0):
    return tgt.at[idx].add(src)

def _segment_sum(src, seg, n):
    return jax.ops.segment_sum(src, seg, n)
kernel_name = 'mk_xattn_ffn_d1_seqx_r4_ebafc8'

def setup_inputs(seed: int=0):
    np.random.seed(seed)
    _w = jnp.asarray

    def _rec_inputs():
        import jax
        import jax.numpy as jnp
        _rk = jax.random.key(seed)
        x = 0.002226 + 0.9996 * jax.random.normal(jax.random.fold_in(_rk, 1), (32, 128, 256), jnp.float32)
        _lenS = 128 - jax.random.randint(jax.random.fold_in(_rk, 7), (32,), 0, max(1, 128 // 4) + 1, jnp.int32)
        _lenS2 = 128 - jax.random.randint(jax.random.fold_in(_rk, 8), (32,), 0, max(1, 128 // 4) + 1, jnp.int32)
        _ctx_1024P = jax.random.normal(jax.random.fold_in(_rk, 11), (32, 16, 256), jnp.float32)
        _ctx_1024c = jax.random.dirichlet(jax.random.fold_in(_rk, 511), 0.3 * jnp.ones((16,), jnp.float32), (32, 128))
        _ctx_1024t = jnp.einsum('bsk,bkd->bsd', _ctx_1024c, _ctx_1024P)
        _ctx_1024t = _ctx_1024t * jax.lax.rsqrt(jnp.mean(jnp.square(_ctx_1024t)) + 1e-12) * 0.953939
        ctx_1024 = -0.000125008 + 0.999885 * (_ctx_1024t + 0.3 * jax.random.normal(jax.random.fold_in(_rk, 611), (32, 128, 256), jnp.float32))
        return (x, ctx_1024)
    x, ctx_1024 = _rec_inputs()

    def _L0_xattn_setup():
        import jax, jax.numpy as jnp
        import numpy as np
        EPS = 1e-05

        def layer_norm(x, g, b):
            mu = jnp.mean(x, axis=-1, keepdims=True)
            var = jnp.var(x, axis=-1, keepdims=True)
            return (x - mu) * jax.lax.rsqrt(var + EPS) * g + b
        key = jax.random.key(seed)
        ks = jax.random.split(key, 8)
        dim, heads, dim_head = (256, 16, 64)
        inner = heads * dim_head
        b, n, m = (8, 1024, 64)
        s = dim ** (-0.5)
        return {'x': jax.random.normal(ks[0], (b, n, dim), jnp.float32), 'latents': jax.random.normal(ks[1], (b, m, dim), jnp.float32), 'ln_m_g': jnp.ones((dim,), jnp.float32), 'ln_m_b': jnp.zeros((dim,), jnp.float32), 'ln_l_g': jnp.ones((dim,), jnp.float32), 'ln_l_b': jnp.zeros((dim,), jnp.float32), 'Wq': jax.random.normal(ks[2], (dim, inner), jnp.float32) * s, 'Wkv': jax.random.normal(ks[3], (dim, 2 * inner), jnp.float32) * s, 'Wout': jax.random.normal(ks[4], (inner, dim), jnp.float32) * s}
    _L0_xattn_all = _L0_xattn_setup()
    _L0_xattn_in = {k: v for k, v in _L0_xattn_all.items() if k in ('ln_m_g', 'ln_m_b', 'ln_l_g', 'ln_l_b', 'Wq', 'Wkv', 'Wout')}
    del _L0_xattn_all

    def _L0_ffn_setup():
        import jax, jax.numpy as jnp
        import numpy as np
        E, D, F = (8, 256, 1024)
        LN_EPS = 1e-05
        key = jax.random.key(seed)
        k = jax.random.split(key, 8)
        x = jax.random.normal(k[0], (4, 512, D), jnp.float32)
        centroids = jax.random.normal(k[1], (E, D), jnp.float32) * 0.1
        ln_g = jnp.ones((E, D), jnp.float32)
        ln_b = jnp.zeros((E, D), jnp.float32)
        w1 = jax.random.normal(k[2], (E, F, D), jnp.float32) * (1.0 / np.sqrt(D))
        b1 = jnp.zeros((E, F), jnp.float32)
        w2 = jax.random.normal(k[3], (E, D, F), jnp.float32) * (1.0 / np.sqrt(F))
        b2 = jnp.zeros((E, D), jnp.float32)
        return {'input_features': x, 'centroids': centroids, 'ln_g': ln_g, 'ln_b': ln_b, 'w1': w1, 'b1': b1, 'w2': w2, 'b2': b2}
    _L0_ffn_all = _L0_ffn_setup()
    _L0_ffn_in = {k: v for k, v in _L0_ffn_all.items() if k in ('centroids', 'ln_g', 'ln_b', 'w1', 'b1', 'w2', 'b2')}
    del _L0_ffn_all
    return {'x': x, 'ctx_1024': ctx_1024, 'L0_xattn_ln_m_g': _L0_xattn_in['ln_m_g'], 'L0_xattn_ln_m_b': _L0_xattn_in['ln_m_b'], 'L0_xattn_ln_l_g': _L0_xattn_in['ln_l_g'], 'L0_xattn_ln_l_b': _L0_xattn_in['ln_l_b'], 'L0_xattn_Wq': _L0_xattn_in['Wq'], 'L0_xattn_Wkv': _L0_xattn_in['Wkv'], 'L0_xattn_Wout': _L0_xattn_in['Wout'], 'L0_ffn_centroids': _L0_ffn_in['centroids'], 'L0_ffn_ln_g': _L0_ffn_in['ln_g'], 'L0_ffn_ln_b': _L0_ffn_in['ln_b'], 'L0_ffn_w1': _L0_ffn_in['w1'], 'L0_ffn_b1': _L0_ffn_in['b1'], 'L0_ffn_w2': _L0_ffn_in['w2'], 'L0_ffn_b2': _L0_ffn_in['b2']}

def reference(x, ctx_1024, L0_xattn_ln_m_g, L0_xattn_ln_m_b, L0_xattn_ln_l_g, L0_xattn_ln_l_b, L0_xattn_Wq, L0_xattn_Wkv, L0_xattn_Wout, L0_ffn_centroids, L0_ffn_ln_g, L0_ffn_ln_b, L0_ffn_w1, L0_ffn_b1, L0_ffn_w2, L0_ffn_b2):
    import jax
    import jax.numpy as jnp

    def _L0_xattn_ref(x, latents, ln_m_g, ln_m_b, ln_l_g, ln_l_b, Wq, Wkv, Wout):
        import jax, jax.numpy as jnp
        import numpy as np
        EPS = 1e-05

        def layer_norm(x, g, b):
            mu = jnp.mean(x, axis=-1, keepdims=True)
            var = jnp.var(x, axis=-1, keepdims=True)
            return (x - mu) * jax.lax.rsqrt(var + EPS) * g + b
        heads, dim_head = (16, 64)
        scale = dim_head ** (-0.5)
        x = layer_norm(x, ln_m_g, ln_m_b)
        lat = layer_norm(latents, ln_l_g, ln_l_b)
        b, m, _ = lat.shape
        q = lat @ Wq
        kv_input = jnp.concatenate([x, lat], axis=1)
        kv = kv_input @ Wkv
        k, v = jnp.split(kv, 2, axis=-1)

        def split_heads(t):
            return t.reshape(t.shape[0], t.shape[1], heads, dim_head).transpose(0, 2, 1, 3)
        q, k, v = (split_heads(q), split_heads(k), split_heads(v))
        dots = jnp.einsum('bhid,bhjd->bhij', q, k) * scale
        attn = jax.nn.softmax(dots, axis=-1)
        out = jnp.einsum('bhij,bhjd->bhid', attn, v)
        out = out.transpose(0, 2, 1, 3).reshape(b, m, heads * dim_head)
        return out @ Wout

    def _L0_ffn_ref(input_features, centroids, ln_g, ln_b, w1, b1, w2, b2):
        import jax, jax.numpy as jnp
        import numpy as np
        E, D, F = (8, 256, 1024)
        LN_EPS = 1e-05
        x = input_features.reshape(-1, D)
        aff = jax.lax.stop_gradient(x) @ centroids.T
        assign = jnp.argmax(aff, axis=1)
        onehot = jax.nn.one_hot(assign, E, dtype=x.dtype)
        mu = jnp.mean(x, axis=-1, keepdims=True)
        var = jnp.mean((x - mu) ** 2, axis=-1, keepdims=True)
        xhat = (x - mu) * jax.lax.rsqrt(var + LN_EPS)
        xn = xhat[None, :, :] * ln_g[:, None, :] + ln_b[:, None, :]
        h = jax.nn.relu(jnp.einsum('etd,efd->etf', xn, w1) + b1[:, None, :])
        y = x[None, :, :] + jnp.einsum('etf,edf->etd', h, w2) + b2[:, None, :]
        alpha = jax.nn.sigmoid(x @ centroids.T)
        a = alpha.T[:, :, None]
        gated = a * y + (1.0 - a) * x[None, :, :]
        out = jnp.einsum('te,etd->td', onehot, gated)
        return out.reshape(input_features.shape)
    x = x + _L0_xattn_ref(ctx_1024, _layernorm(x, axis=-1), L0_xattn_ln_m_g, L0_xattn_ln_m_b, L0_xattn_ln_l_g, L0_xattn_ln_l_b, L0_xattn_Wq, L0_xattn_Wkv, L0_xattn_Wout)
    x = x + _L0_ffn_ref(_layernorm(x, axis=-1), L0_ffn_centroids, L0_ffn_ln_g, L0_ffn_ln_b, L0_ffn_w1, L0_ffn_b1, L0_ffn_w2, L0_ffn_b2)
    return x

_drawn_inputs = setup_inputs


def setup_inputs(seed=0):
    import zlib

    import numpy as np

    out = dict(_drawn_inputs(seed))
    spreads = {'L0_xattn_ln_m_g': (1.0, 0.2),
     'L0_xattn_ln_m_b': (0.0, 0.1),
     'L0_xattn_ln_l_g': (1.0, 0.2),
     'L0_xattn_ln_l_b': (0.0, 0.1),
     'L0_ffn_ln_g': (1.0, 0.2),
     'L0_ffn_ln_b': (0.0, 0.294),
     'L0_ffn_b1': (0.0, 0.291),
     'L0_ffn_b2': (0.0, 0.1)}
    factors = {}
    for name, (base, spread) in spreads.items():
        noise = np.random.default_rng([zlib.crc32(name.encode()), seed]).standard_normal(out[name].shape)
        drawn = base * np.exp(spread * noise) if base else spread * noise
        out[name] = jnp.asarray(drawn.astype(out[name].dtype))
    for name, factor in factors.items():
        out[name] = (out[name] * factor).astype(out[name].dtype)
    return out
```

```python
from contextlib import ExitStack

import concourse.bass as bass
from concourse import mybir

F32 = mybir.dt.float32
F32R = mybir.dt.float32r
I32 = mybir.dt.int32
ACT = mybir.ActivationFunctionType
ALU = mybir.AluOpType
AXIS_X = mybir.AxisListType.X

P = 128
DH = 64
EPS = 1e-5
BANK = 512
OUT_OF_RANGE = 1 << 20

COL_S1, COL_T1, COL_S2, COL_T2, COL_ALPHA, COL_TOKEN = range(256, 262)
ROW = 264

PASSES = ((0, 0), (0, 1), (1, 0))


def plan_jobs(n_batches):
    before = [("ln", 0, 0), ("ln", 1, 0)]
    before += [("q", 0, m) for m in range(4)] + [("k", 0, m) for m in range(4)] + [("v", 0, m) for m in range(4)]
    beside = []
    for b in range(n_batches):
        work = []
        if b % 2 == 1 and b + 1 < n_batches:
            work += [("q", (b + 1) // 2, m) for m in range(4)]
        if b + 1 < n_batches:
            work += [("k", b + 1, m) for m in range(4)] + [("v", b + 1, m) for m in range(4)]
        if b % 2 == 0 and b + 2 < n_batches:
            work += [("ln", b + 2, 0), ("ln", b + 3, 0)]
        for s in range(4):
            part = work[len(work) * s // 4:len(work) * (s + 1) // 4]
            if b >= 1 and s >= 1:
                part = part[:1] + [(("wout", "zt", "aff")[s - 1], b - 1, 0)] + part[1:]
            beside.append(part)
    after = [("wout", n_batches - 1, 0), ("zt", n_batches - 1, 0), ("aff", n_batches - 1, 0)]
    return before, beside, after


def build(nc, x, ctx_in, ln_pack, w_q, w_kv, w_out, centroids_t, consts, experts, b2, out):
    n_batches, _, d_model = x.shape
    inner = w_q.shape[1]
    n_experts = centroids_t.shape[2]

    d_ff = (experts.shape[2] - 12) // 4
    KC = d_model // P
    HC = inner // P
    FC = d_ff // P
    n_tiles = n_batches
    n_slots = n_tiles + n_experts - 1
    n_quads = n_batches * 4
    before, beside, after = plan_jobs(n_batches)
    all_jobs = before + [j for part in beside for j in part] + after
    number = {job: i for i, job in enumerate(all_jobs)}

    sorted_rows = nc.dram_tensor("sorted_rows", [n_slots * P, ROW], F32, kind="Internal").ap()

    with ExitStack() as top:
        def sem(name):
            return top.enter_context(nc.semaphore(name))

        def sbuf(scope, name, shape, dtype=F32):
            return scope.enter_context(nc.sbuf_tensor(name, shape, dtype))

        psum = top.enter_context(nc.psum_tensor("psum", [P, 8, BANK], F32))
        rows = sbuf(top, "rows", [P, n_tiles, ROW])
        ident = sbuf(top, "ident", [P, P])
        lower_ones = sbuf(top, "lower_ones", [P, 2, P])
        tables = sbuf(top, "tables", [P, 32 + 64 + 64])
        prefix8 = sbuf(top, "prefix8", [P, 8, 8])
        onehot = sbuf(top, "onehot", [P, n_tiles, n_experts])
        counts = sbuf(top, "counts", [P, n_tiles + 1, n_experts])
        best = sbuf(top, "best", [P, n_tiles])

        with ExitStack() as a:
            w_split = [sbuf(a, f"w_{h}", [P, KC, 3 * inner], F32R) for h in ("hi", "lo")]
            kv_t = [sbuf(a, f"kv_t_{h}", [P, KC, 4, 2 * P], F32R) for h in ("hi", "lo")]
            w_o = sbuf(a, "w_o", [P, HC, d_model])
            q_t = sbuf(a, "q_t", [P, 2, HC, 2 * P])
            k_t = sbuf(a, "k_t", [P, 2, HC, 2 * P])
            v_n = sbuf(a, "v_n", [P, 2, 2, inner])
            y_t = sbuf(a, "y_t", [P, 2, KC, 2, P])
            NPROB = 5
            prob = sbuf(a, "prob", [P, NPROB, 2, 2 * P])
            NPT = 4
            prob_t = sbuf(a, "prob_t", [P, NPT, 2, 2, P])
            head_out = sbuf(a, "head_out", [P, 2, HC, P])
            NX, NCTX = 6, 4
            x_in = sbuf(a, "x_in", [P, NX, d_model])
            c_in = sbuf(a, "c_in", [P, NCTX, d_model])
            normed = sbuf(a, "normed", [P, 4, d_model])
            z_buf = sbuf(a, "z_buf", [P, d_model])
            z_t = sbuf(a, "z_t", [P, KC, P])
            cent = sbuf(a, "cent", [P, KC, n_experts])
            ln_w = sbuf(a, "ln_w", [P, 4, KC])
            stats = sbuf(a, "stats", [P, 4, 6])
            mean_var = sbuf(a, "mean_var", [P, 4, 2])
            ln_scale = sbuf(a, "ln_scale", [P, 2, 4])
            ln_shift = sbuf(a, "ln_shift", [P, 2, 4])
            tmp_v = sbuf(a, "tmp_v", [P, 4])
            var_eps = sbuf(a, "var_eps", [P, 4])
            minus_half = sbuf(a, "minus_half", [P, 4])
            neg_max = sbuf(a, "neg_max", [P, 8, 2])
            prob_sum = sbuf(a, "prob_sum", [P, 8, 2])
            inv_sum = sbuf(a, "inv_sum", [P, 8, 2])
            stats_z = sbuf(a, "stats_z", [P, 2, 6])
            mv_z = sbuf(a, "mv_z", [P, 2, 2])
            aff = sbuf(a, "aff", [P, 2, n_experts])
            rank_w = sbuf(a, "rank_w", [P, n_experts])
            rank_m = sbuf(a, "rank_m", [P, 1])

            s_const = sem("s_const")
            s_in = [sem("s_in0"), sem("s_in1")]
            s_w = [sem(f"s_w{i}") for i in range(3)]
            s_wo = sem("s_wo")
            s_whi = sem("s_whi")
            s_wlo = sem("s_wlo")
            s_lnp = sem("s_lnp")
            s_mv = sem("s_mv")
            s_mv1 = sem("s_mv1")
            s_mv2 = sem("s_mv2")
            s_st1 = sem("s_st1")
            s_st2 = sem("s_st2")
            s_pool = sem("s_pool")
            s_nrm = sem("s_nrm")
            s_job = sem("s_job")
            s_bank = [sem("s_bank0"), sem("s_bank1")]
            s_hi = sem("s_hi")
            s_lo = sem("s_lo")
            s_score = sem("s_score")
            s_max = sem("s_max")
            s_exp = sem("s_exp")
            s_inv = sem("s_inv")
            s_soft = sem("s_soft")
            s_tr = sem("s_tr")
            s_pt = sem("s_pt")
            s_pv = sem("s_pv")
            s_ho = sem("s_ho")
            s_z = sem("s_z")
            s_dve = sem("s_dve")
            s_fill = sem("s_fill")
            s_pad = sem("s_pad")
            filler = sbuf(a, "filler", [P, ROW])

            stage = rows[:, :, :].rearrange("p t c -> p (t c)")
            w_raw = sbuf(a, "w_raw", [P, KC, 3 * inner]) if n_tiles * ROW < KC * 3 * inner else \
                stage[:, 0:KC * 3 * inner].rearrange("p (c n) -> p c n", c=KC)

            block = a.enter_context(nc.Block())

            def unit_bank(n):
                return n % 3

            def tr_bank(n):
                return 3 + n % 2

            OUT_BANK = 5

            def job_bank(j):
                return psum[:, 6 + j % 2, :]

            def wait_read(eng, job):
                j = number[job]
                eng.wait_ge(s_bank[j % 2], j // 2 + 1)

            def wait_job(eng, job):
                eng.wait_ge(s_job, number[job] + 1)

            def unit_heads(n):
                quad, parity = n // 2, n % 2
                h0 = 4 * (quad % 4) + parity
                return quad // 4, (h0, h0 + 2)

            @block.sync
            def _(sp):
                def load_pair(g):
                    if g >= 2:
                        sp.wait_ge(s_nrm, g - 1)
                    if g >= 3:
                        sp.wait_ge(s_z, 2 * (g - 3) + 2)
                    b = 2 * g
                    sp.dma_start(x_in[:, b % NX:b % NX + 2, :],
                                 x[b:b + 2].rearrange("b p d -> p b d")).then_inc(s_in[g % 2], 16)
                    sp.dma_start(c_in[:, b % NCTX:b % NCTX + 2, :],
                                 ctx_in[b:b + 2].rearrange("b p d -> p b d")).then_inc(s_in[g % 2], 16)

                load_pair(0)
                sp.dma_start(ident[:], consts[:, 0:P]).then_inc(s_const, 16)
                sp.dma_start(ln_w[:], ln_pack).then_inc(s_const, 16)
                for i, src in enumerate((w_q, w_kv[:, 0:inner], w_kv[:, inner:2 * inner])):
                    sp.dma_start(w_raw[:, :, i * inner:(i + 1) * inner],
                                 src.rearrange("(c p) n -> p c n", p=P)).then_inc(s_w[i], 16)
                load_pair(1)
                sp.dma_start(w_o[:], w_out.rearrange("(c p) n -> p c n", p=P)).then_inc(s_wo, 16)
                sp.dma_start(lower_ones[:], consts[:, P:3 * P].rearrange("p (a b) -> p a b", a=2)).then_inc(s_const, 16)
                sp.dma_start(tables[:], consts[:, 3 * P:3 * P + 160]).then_inc(s_const, 16)
                sp.dma_start(prefix8[:], consts[:, 3 * P + 160:3 * P + 224].rearrange("p (a b) -> p a b", a=8)).then_inc(s_const, 16)
                sp.dma_start(cent[:], centroids_t).then_inc(s_const, 16)
                sp.wait_ge(s_pad, 2)
                sp.dma_start(sorted_rows.rearrange("(s p) c -> p s c", p=P),
                             filler[:, None, :].to_broadcast([P, n_slots, ROW])).then_inc(s_fill, 16)
                for g in range(2, n_batches // 2):
                    load_pair(g)
                sp.wait_ge(s_fill, 16)

            @block.tensor
            def _(pe):
                def run_job(job):
                    kind, b, m = job
                    j = number[job]
                    bank = job_bank(j)
                    if j >= 2:
                        pe.wait_ge(s_bank[j % 2], j // 2)
                    if kind == "ln":
                        pe.wait_ge(s_nrm, b // 2 + 1)
                        for c in range(KC):
                            for side in range(2):
                                last = pe.transpose(bank[:, (2 * c + side) * P:(2 * c + side + 1) * P],
                                                    normed[:, 2 * side + b % 2, c * P:(c + 1) * P], ident[:])
                    elif kind in "qk":
                        first_b = 2 * b if kind == "q" else b
                        pe.wait_ge(s_hi, (2 * b + 2) if kind == "q" else b + 1)
                        pe.wait_ge(s_lo, (2 * b + 2) if kind == "q" else b + 1)
                        slot = first_b % 4
                        for cc in range(2):
                            col = (inner if kind == "k" else 0) + (2 * m + cc) * P
                            for i, (hw, hx) in enumerate(PASSES):
                                for c in range(KC):
                                    tokens = (kv_t[hx][:, c, slot, :] if kind == "k" else
                                              kv_t[hx][:, c, slot:slot + 2, P:2 * P])
                                    dst = bank[:, cc * 2 * P:(cc + 1) * 2 * P]
                                    if kind == "q":
                                        dst = dst.rearrange("p (a t) -> p a t", a=2)
                                    last = pe.matmul(dst, w_split[hw][:, c, col:col + P], tokens,
                                                     start=(i == 0 and c == 0), stop=(i == 2 and c == KC - 1))
                    elif kind == "v":
                        side, half = m // 2, m % 2
                        slot = b % 4
                        for i, (hx, hw) in enumerate(PASSES):
                            for c in range(KC):
                                last = pe.matmul(bank, kv_t[hx][:, c, slot, side * P:(side + 1) * P],
                                                 w_split[hw][:, c, 2 * inner + half * BANK:2 * inner + (half + 1) * BANK],
                                                 start=(i == 0 and c == 0), stop=(i == 2 and c == KC - 1))
                    elif kind == "wout":
                        pe.wait_ge(s_ho, 2 * b + 2)
                        for c in range(HC):
                            last = pe.matmul(bank[:, 0:d_model], head_out[:, b % 2, c, :], w_o[:, c, :],
                                             start=(c == 0), stop=(c == HC - 1))
                    elif kind == "zt":
                        pe.wait_ge(s_z, b + 1)
                        for c in range(KC):
                            last = pe.transpose(bank[:, c * P:(c + 1) * P], z_buf[:, c * P:(c + 1) * P], ident[:])
                    else:
                        wait_read(pe, ("zt", b, 0))
                        for c in range(KC):
                            last = pe.matmul(bank[:, 0:n_experts], z_t[:, c, :], cent[:, c, :],
                                             start=(c == 0), stop=(c == KC - 1))
                    last.then_inc(s_job, 1)

                def scores(quad):
                    b = quad // 4
                    if quad % 4 == 0:
                        wait_read(pe, ("k", b, 3))
                        wait_read(pe, ("k", b, 2))
                        wait_read(pe, ("q", b // 2, 3))
                        wait_read(pe, ("q", b // 2, 2))
                    for n in (2 * quad, 2 * quad + 1):
                        if n >= 3:
                            pe.wait_ge(s_exp, 2 * (n - 3) + 2)
                    for i in range(2):
                        for n in (2 * quad, 2 * quad + 1):
                            h = unit_heads(n)[1][i]
                            lo = DH * (h % 2)
                            ins = pe.matmul(psum[:, unit_bank(n), i * 2 * P:(i + 1) * 2 * P],
                                            q_t[lo:lo + DH, (b // 2) % 2, h // 2, (b % 2) * P:(b % 2 + 1) * P],
                                            k_t[lo:lo + DH, b % 2, h // 2, :], start=True, stop=True)
                            if i == 1:
                                ins.then_inc(s_score, 1)

                def transposes(n):
                    pe.wait_ge(s_soft, n + 1)
                    if n >= 2:
                        pe.wait_ge(s_pt, n - 1)
                    for i in range(2):
                        for side in range(2):
                            last = pe.transpose(psum[:, tr_bank(n), (2 * i + side) * P:(2 * i + side + 1) * P],
                                                prob[:, n % NPROB, i, side * P:(side + 1) * P], ident[:])
                    last.then_inc(s_tr, 1)

                def outputs(quad):
                    b = quad // 4
                    if quad % 4 == 0:
                        wait_read(pe, ("v", b, 3))
                        wait_read(pe, ("v", b, 2))
                    pe.wait_ge(s_pt, 2 * quad + 2)
                    if quad % 2 == 0 and quad >= 2:
                        pe.wait_ge(s_ho, quad // 2)
                    for i in range(2):
                        for side in range(2):
                            for n in (2 * quad, 2 * quad + 1):
                                h = unit_heads(n)[1][i]
                                lo = DH * (h % 2)
                                slot = (h // 2) % 4
                                last = pe.matmul(psum[lo:lo + DH, OUT_BANK, slot * P:(slot + 1) * P],
                                                 v_n[:, b % 2, side, h * DH:(h + 1) * DH],
                                                 prob_t[:, n % NPT, i, side, :],
                                                 start=(side == 0), stop=(side == 1))
                    last.then_inc(s_pv, 1)

                pe.wait_ge(s_const, 6 * 16)
                for job in before[:2]:
                    run_job(job)
                pe.wait_ge(s_whi, 3 * KC * 2)
                pe.wait_ge(s_wlo, 3 * KC)
                pe.wait_ge(s_wo, 16)
                for job in before[2:]:
                    run_job(job)
                for t in range(n_quads + 1):
                    jobs = beside[t] if t < n_quads else []
                    if t < n_quads:
                        scores(t)
                    for job in jobs[:1]:
                        run_job(job)
                    if t >= 1:
                        transposes(2 * t - 2)
                        transposes(2 * t - 1)
                    for job in jobs[1:2]:
                        run_job(job)
                    if t >= 1:
                        outputs(t - 1)
                    for job in jobs[2:]:
                        run_job(job)
                for job in after:
                    run_job(job)

            @block.scalar
            def _(act):
                def normalise(g):
                    act.wait_ge(s_lnp, g + 1)
                    if g >= 1:
                        wait_job(act, ("ln", 2 * g - 1, 0))
                    for j in range(4):
                        side, b = j // 2, 2 * g + j % 2
                        src = c_in[:, b % NCTX, :] if side == 0 else x_in[:, b % NX, :]
                        last = act.activation(normed[:, j, :], src, ACT.Identity,
                                              bias=ln_shift[:, g % 2, j:j + 1], scale=ln_scale[:, g % 2, j:j + 1])
                    last.then_inc(s_nrm, 1)

                def read_job(job):
                    kind, b, m = job
                    if kind not in ("ln", "q", "k", "v"):
                        return
                    j = number[job]
                    bank = job_bank(j)
                    wait_job(act, job)
                    if kind == "ln":
                        if b >= 2:
                            act.wait_ge(s_lo, b - 1)
                        for c in range(KC):
                            for side in range(2):
                                last = act.activation(y_t[:, b % 2, c, side, :],
                                                      bank[:, (2 * c + side) * P:(2 * c + side + 1) * P], ACT.Identity,
                                                      bias=ln_w[:, 2 * side + 1, c:c + 1], scale=ln_w[:, 2 * side, c:c + 1])
                    elif kind == "q":
                        if b >= 2:
                            act.wait_ge(s_score, 16 * (b - 1))
                        last = act.activation(q_t[:, b % 2, 2 * m:2 * m + 2, :].rearrange("p c t -> p (c t)"), bank,
                                              ACT.Copy, scale=DH ** -0.5)
                    elif kind == "k":
                        if b >= 2:
                            act.wait_ge(s_score, 8 * (b - 1))
                        last = act.activation(k_t[:, b % 2, 2 * m:2 * m + 2, :].rearrange("p c t -> p (c t)"), bank, ACT.Copy)
                    else:
                        if b >= 2:
                            act.wait_ge(s_pv, 4 * (b - 1))
                        last = act.activation(v_n[:, b % 2, m // 2, (m % 2) * BANK:(m % 2 + 1) * BANK], bank, ACT.Copy)
                    last.then_inc(s_bank[j % 2], 1)

                def exponentials(n):
                    act.wait_ge(s_max, n + 1)
                    if n >= NPROB:
                        act.wait_ge(s_tr, n - NPROB + 1)
                    for i in range(2):
                        act.activation(prob[:, n % NPROB, i, :], psum[:, unit_bank(n), i * 2 * P:(i + 1) * 2 * P], ACT.Exp,
                                       bias=neg_max[:, n % 8, i:i + 1],
                                       accum_out=prob_sum[:, n % 8, i:i + 1]).then_inc(s_exp, 1)

                def copy_outputs(half):
                    act.wait_ge(s_pv, 2 * half + 2)
                    b = half // 2
                    if b >= 2 and half % 2 == 0:
                        wait_job(act, ("wout", b - 2, 0))
                    act.activation(head_out[:, b % 2, 4 * (half % 2):4 * (half % 2) + 4, :].rearrange("p c t -> p (c t)"),
                                   psum[:, OUT_BANK, :], ACT.Copy).then_inc(s_ho, 1)

                def norm_x1(b):
                    act.wait_ge(s_st1, b + 1)
                    if b >= 1:
                        wait_job(act, ("zt", b - 1, 0))
                        act.wait_ge(s_mv2, b)
                    act.activation(z_buf[:], rows[:, b, 0:d_model], ACT.Identity, bias=rows[:, b, COL_T1:COL_T1 + 1],
                                   scale=rows[:, b, COL_S1:COL_S1 + 1]).then_inc(s_z, 1)

                act.wait_ge(s_const, 6 * 16)
                normalise(0)
                for job in before:
                    read_job(job)
                for t in range(n_quads + 1):
                    jobs = beside[t] if t < n_quads else []
                    if t < n_quads:
                        exponentials(2 * t)
                    for job in jobs[:1]:
                        read_job(job)
                    if t < n_quads:
                        exponentials(2 * t + 1)
                    for job in jobs[1:2]:
                        read_job(job)
                    if t >= 2 and t % 2 == 0:
                        copy_outputs(t // 2 - 1)
                    for job in jobs[2:]:
                        read_job(job)
                    for kind, b, _ in jobs:
                        if kind == "wout":
                            norm_x1(b)
                    b = t // 4
                    if t % 8 == 1 and b + 2 < n_batches:
                        normalise(b // 2 + 1)
                norm_x1(n_batches - 1)

            @block.vector
            def _(dve):
                chained = [0]

                def then_next(ins):
                    chained[0] += 1
                    ins.then_inc(s_dve, 1)
                    dve.wait_ge(s_dve, chained[0])

                def layer_norm_stats(g):
                    dve.wait_ge(s_in[g % 2], 32 * (g // 2 + 1))
                    if g >= 1:
                        dve.wait_ge(s_lnp, g)
                    for j in range(4):
                        side, b = j // 2, 2 * g + j % 2
                        src = c_in[:, b % NCTX, :] if side == 0 else x_in[:, b % NX, :]
                        last = dve.bn_stats(stats[:, j, :], src)
                    then_next(last)
                    for j in range(4):
                        last = dve.bn_aggr(mean_var[:, j, :], stats[:, j, :])
                    last.then_inc(s_mv, 1)

                def maxima(n):
                    dve.wait_ge(s_score, n + 1)
                    dve.tensor_reduce(neg_max[:, n % 8, :], psum[:, unit_bank(n), :].rearrange("p (i j) -> p i j", i=2),
                                      AXIS_X, ALU.max, negate=True).then_inc(s_max, 1)

                def inverse_sums(n):
                    dve.wait_ge(s_exp, 2 * n + 2)
                    dve.reciprocal(inv_sum[:, n % 8, :], prob_sum[:, n % 8, :]).then_inc(s_inv, 1)

                def copy_transposed(n):
                    dve.wait_ge(s_tr, n + 1)
                    if n >= NPT:
                        dve.wait_ge(s_pv, (n - NPT) // 2 + 1)
                    dve.tensor_copy(prob_t[:, n % NPT].rearrange("p i s t -> p (i s t)"), psum[:, tr_bank(n), :]).then_inc(s_pt, 1)

                def read_job(job):
                    kind, b, m = job
                    j = number[job]
                    bank = job_bank(j)
                    if kind == "ln":
                        wait_read(dve, job)
                        if b >= 4:
                            wait_job(dve, ("v", b - 4, 3))
                        dve.tensor_copy(kv_t[0][:, :, b % 4, :].rearrange("p c (s t) -> p c s t", s=2), y_t[:, b % 2]).then_inc(s_hi, 1)
                    elif kind == "wout":
                        wait_job(dve, job)
                        if b == 0:
                            dve.wait_ge(s_wlo, 3 * KC)
                        x1 = rows[:, b, 0:d_model]
                        ins = dve.tensor_tensor(x1, bank[:, 0:d_model], x_in[:, b % NX, :], ALU.add)
                        ins.then_inc(s_bank[j % 2], 1)
                        dve.wait_ge(s_bank[j % 2], j // 2 + 1)
                        then_next(dve.bn_stats(stats_z[:, 0, :], x1))
                        if b >= 1:
                            dve.wait_ge(s_st1, b)
                        dve.bn_aggr(mv_z[:, 0, :], stats_z[:, 0, :]).then_inc(s_mv1, 1)
                    elif kind == "zt":
                        wait_job(dve, job)
                        if b >= 1:
                            wait_job(dve, ("aff", b - 1, 0))
                        dve.tensor_copy(z_t[:].rearrange("p c t -> p (c t)"), bank[:, 0:KC * P]).then_inc(s_bank[j % 2], 1)
                        dve.wait_ge(s_z, b + 1)
                        then_next(dve.bn_stats(stats_z[:, 1, :], z_buf[:]))
                        if b >= 1:
                            dve.wait_ge(s_st2, b)
                        dve.bn_aggr(mv_z[:, 1, :], stats_z[:, 1, :]).then_inc(s_mv2, 1)
                    elif kind == "aff":
                        wait_job(dve, job)
                        scores_b, same = aff[:, 0, :], aff[:, 1, :]
                        dve.tensor_copy(scores_b, bank[:, 0:n_experts]).then_inc(s_bank[j % 2], 1)
                        dve.wait_ge(s_bank[j % 2], j // 2 + 1)
                        then_next(dve.tensor_reduce(best[:, b:b + 1], scores_b, AXIS_X, ALU.max))
                        then_next(dve.tensor_scalar(same, scores_b, best[:, b:b + 1], None, ALU.is_equal))
                        then_next(dve.tensor_tensor(rank_w[:], same, tables[:, 0:n_experts], ALU.mult))
                        then_next(dve.tensor_reduce(rank_m[:], rank_w[:], AXIS_X, ALU.max))
                        then_next(dve.tensor_scalar(onehot[:, b, :], rank_w[:], rank_m[:, 0:1], None, ALU.is_equal))
                        then_next(dve.tensor_tensor(counts[:, b + 1, :], counts[:, b, :], onehot[:, b, :], ALU.add))

                then_next(dve.memset(counts[:, 0, :], 0.0))
                layer_norm_stats(0)
                for i in range(3):
                    dve.wait_ge(s_w[i], 16)
                    for c in range(KC):
                        cols = slice(i * inner, (i + 1) * inner)
                        raw, hi, lo = w_raw[:, c, cols], w_split[0][:, c, cols], w_split[1][:, c, cols]
                        dve.tensor_copy(hi, raw).then_inc(s_whi, 1)
                        dve.wait_ge(s_whi, 2 * (i * KC + c) + 1)
                        half = inner // 2
                        dve.tensor_tensor(lo[:, 0:half], raw[:, 0:half], hi[:, 0:half], ALU.subtract).then_inc(s_whi, 1)
                for job in before:
                    read_job(job)
                dve.wait_ge(s_const, 6 * 16)
                for t in range(n_quads + 1):
                    if t < n_quads:
                        maxima(2 * t)
                        maxima(2 * t + 1)
                    if t >= 1:
                        copy_transposed(2 * t - 2)
                        copy_transposed(2 * t - 1)
                    if t < n_quads:
                        inverse_sums(2 * t)
                        inverse_sums(2 * t + 1)
                        for job in beside[t]:
                            read_job(job)
                    if t % 8 == 0 and t // 4 + 2 < n_batches:
                        layer_norm_stats(t // 8 + 1)
                for job in after:
                    read_job(job)

            @block.gpsimd
            def _(pool):
                def low_half(b):
                    pool.wait_ge(s_hi, b + 1)
                    pool.tensor_tensor(kv_t[1][:, :, b % 4, :].rearrange("p c (s t) -> p c s t", s=2), y_t[:, b % 2],
                                       kv_t[0][:, :, b % 4, :].rearrange("p c (s t) -> p c s t", s=2),
                                       ALU.subtract).then_inc(s_lo, 1)

                def soften(n):
                    pool.wait_ge(s_inv, n + 1)
                    probs = prob[:, n % NPROB]
                    pool.tensor_tensor(probs, probs, inv_sum[:, n % 8, :, None].to_broadcast([P, 2, 2 * P]),
                                       ALU.mult).then_inc(s_soft, 1)

                chained = [0]

                def then_next(ins):
                    chained[0] += 1
                    ins.then_inc(s_pool, 1)
                    pool.wait_ge(s_pool, chained[0])

                def inv_sqrt(dst, var):
                    n = var.shape[1]
                    then_next(pool.tensor_scalar(var_eps[:, 0:n], var, EPS, None, ALU.add))
                    return pool.tensor_tensor(dst, var_eps[:, 0:n], minus_half[:, 0:n], ALU.pow)

                def layer_norm_scales(g):
                    pool.wait_ge(s_mv, g + 1)
                    if g >= 2:
                        pool.wait_ge(s_nrm, g - 1)
                    scale, shift = ln_scale[:, g % 2, :], ln_shift[:, g % 2, :]
                    mean, var = mean_var[:, :, 0], mean_var[:, :, 1]
                    then_next(inv_sqrt(scale, var))
                    then_next(pool.tensor_tensor(tmp_v[:, 0:2], var[:, 2:4], scale[:, 2:4], ALU.mult))
                    then_next(pool.tensor_tensor(tmp_v[:, 2:4], tmp_v[:, 0:2], scale[:, 2:4], ALU.mult))
                    then_next(inv_sqrt(tmp_v[:, 0:2], tmp_v[:, 2:4]))
                    then_next(pool.tensor_tensor(scale[:, 2:4], scale[:, 2:4], tmp_v[:, 0:2], ALU.mult))
                    then_next(pool.tensor_tensor(shift, mean, scale, ALU.mult))
                    pool.tensor_scalar(shift, shift, -1.0, None, ALU.mult).then_inc(s_lnp, 1)

                def row_scales(b, which, s_from, s_to):
                    pool.wait_ge(s_from, b + 1)
                    col = (COL_S1, COL_S2)[which]
                    scale, shift = rows[:, b, col:col + 1], rows[:, b, col + 1:col + 2]
                    then_next(inv_sqrt(scale, mv_z[:, which, 1:2]))
                    then_next(pool.tensor_tensor(shift, mv_z[:, which, 0:1], scale, ALU.mult))
                    pool.tensor_scalar(shift, shift, -1.0, None, ALU.mult).then_inc(s_to, 1)

                then_next(pool.memset(minus_half[:], -0.5))
                layer_norm_scales(0)
                pool.memset(filler[:], 0.0).then_inc(s_pad, 1)
                pool.wait_ge(s_pad, 1)
                pool.memset(filler[:].bitcast(I32)[:, COL_TOKEN:COL_TOKEN + 1], OUT_OF_RANGE).then_inc(s_pad, 1)
                low_half(0)
                low_half(1)
                for i in range(3):
                    for c in range(KC):
                        pool.wait_ge(s_whi, 2 * (i * KC + c) + 1)
                        cols = slice(i * inner + inner // 2, (i + 1) * inner)
                        pool.tensor_tensor(w_split[1][:, c, cols], w_raw[:, c, cols], w_split[0][:, c, cols],
                                           ALU.subtract).then_inc(s_wlo, 1)
                for t in range(n_quads):
                    soften(2 * t)
                    soften(2 * t + 1)
                    for job in beside[t]:
                        if job[0] == "ln":
                            low_half(job[1])
                        if job[0] == "wout":
                            row_scales(job[1], 0, s_mv1, s_st1)
                        if job[0] == "zt":
                            row_scales(job[1], 1, s_mv2, s_st2)
                    if t % 8 == 0 and t // 4 + 2 < n_batches:
                        layer_norm_scales(t // 8 + 1)
                row_scales(n_batches - 1, 0, s_mv1, s_st1)
                row_scales(n_batches - 1, 1, s_mv2, s_st2)

        with ExitStack() as bb:
            NW = 4
            NR = 4
            width = experts.shape[2]
            w_ring = sbuf(bb, "w_ring", [P, NW, width])
            b2_ring = sbuf(bb, "b2_ring", [P, NW, d_model])
            r_ring = sbuf(bb, "r_ring", [P, NR, ROW])
            zz = sbuf(bb, "zz", [P, 2, d_model])
            xhat = sbuf(bb, "xhat", [P, 2, d_model])
            base = sbuf(bb, "base", [P, NR, d_model])
            xn_t = sbuf(bb, "xn_t", [P, 2, KC, P])
            hid_t = sbuf(bb, "hid_t", [P, 2, FC, P])
            upd = sbuf(bb, "upd", [P, 2, d_model])
            fin = sbuf(bb, "fin", [P, NR, d_model])
            over = sbuf(bb, "over", [P, n_experts, n_tiles])
            blocks_e = sbuf(bb, "blocks_e", [P, n_experts])
            pre = sbuf(bb, "pre", [P, n_experts, n_experts])
            start_e = sbuf(bb, "start_e", [P, 2, n_experts])
            total_e = sbuf(bb, "total_e", [P, n_experts])
            place = sbuf(bb, "place", [P, n_tiles, n_experts])
            place_r = sbuf(bb, "place_r", [P, n_tiles])
            place_i = sbuf(bb, "place_i", [P, n_tiles], I32)
            slot_cmp = sbuf(bb, "slot_cmp", [1, n_slots, n_experts - 1])
            slot_f = sbuf(bb, "slot_f", [1, n_slots])
            slot_i = sbuf(bb, "slot_i", [1, n_slots], I32)
            gate = sbuf(bb, "gate", [P, 2, n_tiles])

            r_dve = sem("r_dve")
            r_mm = sem("r_mm")
            r_gate = sem("r_gate")
            r_slot = sem("r_slot")
            r_place = sem("r_place")
            r_scat = sem("r_scat")
            f_w = [sem(f"f_w{i}") for i in range(NW)]
            f_r = [sem(f"f_r{i}") for i in range(NR)]
            f_xh = sem("f_xh")
            f_base = sem("f_base")
            f_t = sem("f_t")
            f_xn = sem("f_xn")
            f_h = sem("f_h")
            f_ha = sem("f_ha")
            f_hd = sem("f_hd")
            f_y = sem("f_y")
            f_o = sem("f_o")
            f_out = [sem(f"f_out{i}") for i in range(NR)]

            block = bb.enter_context(nc.Block())
            RANK_BANK, TOTAL_BANK = 0, 1
            VEC = 2 * KC * d_ff

            def tr_out(s):
                return psum[:, s % 2, :]

            def hid_out(s, half):
                return psum[:, 2 + 2 * (s % 2) + half, :]

            def upd_out(s):
                return psum[:, 6 + s % 2, 0:d_model]

            @block.sync
            def _(sp):
                sp.wait_ge(r_slot, 1)
                for s in range(n_slots):
                    if s >= NW:
                        sp.wait_ge(f_o, s - NW + 1)
                    e = sp.value_load(slot_i[0:1, s:s + 1], min_val=0, max_val=n_experts - 1)
                    sp.dma_start(w_ring[:, s % NW, :], experts[bass.DynSlice(e, 1), :, :].rearrange("o p n -> p (o n)")
                                 ).then_inc(f_w[s % NW], 16)
                    sp.dma_start(b2_ring[:, s % NW, :], b2[bass.DynSlice(e, 1), :].to_broadcast([P, d_model])
                                 ).then_inc(f_w[s % NW], 16)
                    if s == 0:
                        sp.wait_ge(r_scat, 16 * n_tiles)
                    if s >= NR:
                        sp.wait_ge(f_out[s % NR], 16 * (s // NR))
                    sp.dma_start(r_ring[:, s % NR, :], sorted_rows[s * P:(s + 1) * P, :]).then_inc(f_r[s % NR], 16)

            @block.gpsimd
            def _(pool):
                pool.wait_ge(r_place, 1)
                for t in range(n_tiles):
                    pool.indirect_dma_start(out=sorted_rows, out_offset=bass.IndirectOffsetOnAxis(ap=place_i[:, t:t + 1], axis=0),
                                            in_=rows[:, t, :], in_offset=None).then_inc(r_scat, 16)
                for s in range(n_slots):
                    pool.wait_ge(f_o, s + 1)
                    pool.indirect_dma_start(out=out, out_offset=bass.IndirectOffsetOnAxis(
                        ap=r_ring[:, s % NR, COL_TOKEN:COL_TOKEN + 1].bitcast(I32), axis=0),
                        in_=fin[:, s % NR, :], in_offset=None,
                        bounds_check=n_tiles * P - 1, oob_is_err=False).then_inc(f_out[s % NR], 16)
                for i in range(NR):
                    pool.wait_ge(f_out[i], 16 * len(range(i, n_slots, NR)))

            @block.tensor
            def _(pe):
                onehots = onehot[:].rearrange("p t e -> p (t e)")
                earlier = counts[:, 0:n_tiles, :].rearrange("p t e -> p (t e)")
                width_r = n_tiles * n_experts
                pe.matmul(psum[:, RANK_BANK, 0:width_r], lower_ones[:, 0, :], onehots, start=True, stop=False)
                pe.matmul(psum[:, RANK_BANK, 0:width_r], lower_ones[:, 1, :], earlier, start=False, stop=True)
                pe.matmul(psum[:, TOTAL_BANK, 0:n_experts], lower_ones[:, 1, :], counts[:, n_tiles, :],
                          start=True, stop=True).then_inc(r_mm, 1)

                def transposes(s):
                    pe.wait_ge(f_xh, s + 1)
                    if s == 0:
                        pe.wait_ge(r_place, 1)
                    if s >= 2:
                        pe.wait_ge(f_xn, s - 1)
                    for c in range(KC):
                        last = pe.transpose(tr_out(s)[:, c * P:(c + 1) * P], xhat[:, s % 2, c * P:(c + 1) * P], ident[:])
                    last.then_inc(f_t, 1)

                def layer_1(s):
                    pe.wait_ge(f_xn, s + 1)
                    pe.wait_ge(f_w[s % NW], 32 * (s // NW + 1))
                    if s >= 2:
                        pe.wait_ge(f_ha, s - 1)
                        pe.wait_ge(f_hd, s - 1)
                    w1 = w_ring[:, s % NW, 0:KC * d_ff].rearrange("p (c f) -> p c f", c=KC)
                    for f in range(FC):
                        dst = hid_out(s, f // 4)[:, (f % 4) * P:(f % 4 + 1) * P]
                        for c in range(KC):
                            last = pe.matmul(dst, w1[:, c, f * P:(f + 1) * P], xn_t[:, s % 2, c, :],
                                             start=(c == 0), stop=(c == KC - 1))
                        if f % 4 == 3:
                            last.then_inc(f_h, 1)

                def layer_2(s):
                    pe.wait_ge(f_ha, s + 1)
                    if s >= 2:
                        pe.wait_ge(f_o, s - 1)
                    w2 = w_ring[:, s % NW, KC * d_ff:VEC].rearrange("p (f d) -> p f d", f=FC)
                    for f in range(FC):
                        if f == FC // 2:
                            pe.wait_ge(f_hd, s + 1)
                        last = pe.matmul(upd_out(s), hid_t[:, s % 2, f, :], w2[:, f, :], start=(f == 0), stop=(f == FC - 1))
                    last.then_inc(f_y, 1)

                transposes(0)
                transposes(1)
                layer_1(0)
                for s in range(n_slots):
                    if s + 2 < n_slots:
                        transposes(s + 2)
                    if s + 1 < n_slots:
                        layer_1(s + 1)
                    layer_2(s)

            @block.scalar
            def _(act):
                act.activation(gate[:, 0, :], best[:], ACT.Exp, scale=-1.0).then_inc(r_gate, 1)

                def gain_bias(s):
                    act.wait_ge(f_t, s + 1)
                    act.wait_ge(f_w[s % NW], 32 * (s // NW + 1))
                    if s >= 2:
                        act.wait_ge(f_h, 2 * (s - 2) + 2)
                    vec = w_ring[:, s % NW, VEC:VEC + 2 * KC]
                    for c in range(KC):
                        last = act.activation(xn_t[:, s % 2, c, :], tr_out(s)[:, c * P:(c + 1) * P], ACT.Identity,
                                              bias=vec[:, KC + c:KC + c + 1], scale=vec[:, c:c + 1])
                    last.then_inc(f_xn, 1)

                def relu(s):
                    act.wait_ge(f_h, 2 * s + 1)
                    if s >= 2:
                        act.wait_ge(f_y, s - 1)
                    b1 = w_ring[:, s % NW, VEC + 2 * KC:]
                    for f in range(FC // 2):
                        last = act.activation(hid_t[:, s % 2, f, :], hid_out(s, 0)[:, f * P:(f + 1) * P], ACT.Relu,
                                              bias=b1[:, f:f + 1])
                    last.then_inc(f_ha, 1)

                gain_bias(0)
                gain_bias(1)
                for s in range(n_slots):
                    relu(s)
                    if s + 2 < n_slots:
                        gain_bias(s + 2)

            @block.vector
            def _(dve):
                chained = [0]

                def then_next(ins):
                    chained[0] += 1
                    ins.then_inc(r_dve, 1)
                    dve.wait_ge(r_dve, chained[0])

                dve.wait_ge(r_mm, 1)
                then_next(dve.tensor_copy(total_e[:], psum[:, TOTAL_BANK, 0:n_experts]))
                then_next(dve.tensor_tensor(over[:], total_e[:, :, None].to_broadcast([P, n_experts, n_tiles]),
                                            tables[:, None, 32:32 + n_tiles].to_broadcast([P, n_experts, n_tiles]), ALU.is_gt))
                then_next(dve.tensor_reduce(blocks_e[:], over[:], AXIS_X, ALU.add))
                then_next(dve.tensor_tensor(pre[:], prefix8[:], blocks_e[:, None, :].to_broadcast([P, n_experts, n_experts]), ALU.mult))
                then_next(dve.tensor_reduce(start_e[:, 0, :], pre[:], AXIS_X, ALU.add))
                then_next(dve.tensor_tensor(slot_cmp[:], start_e[0:1, 0:1, 1:].to_broadcast([1, n_slots, n_experts - 1]),
                                            tables[0:1, 64:64 + n_slots, None].to_broadcast([1, n_slots, n_experts - 1]), ALU.is_le))
                then_next(dve.tensor_reduce(slot_f[:], slot_cmp[:], AXIS_X, ALU.add))
                dve.tensor_copy(slot_i[:], slot_f[:]).then_inc(r_slot, 1)
                then_next(dve.tensor_scalar(start_e[:, 1, :], start_e[:, 0, :], float(P), None, ALU.mult))
                ranks = psum[:, RANK_BANK, 0:n_tiles * n_experts].rearrange("p (t e) -> p t e", t=n_tiles)
                then_next(dve.tensor_tensor(place[:], ranks, start_e[:, 1:2, :].to_broadcast([P, n_tiles, n_experts]), ALU.add))
                then_next(dve.tensor_tensor(place[:], place[:], onehot[:], ALU.mult))
                then_next(dve.tensor_reduce(place_r[:], place[:], AXIS_X, ALU.add))
                dve.wait_ge(r_gate, 1)
                then_next(dve.tensor_scalar(gate[:, 1, :], gate[:, 0, :], 1.0, None, ALU.add))
                then_next(dve.reciprocal(rows[:, :, COL_ALPHA], gate[:, 1, :]))
                then_next(dve.tensor_copy(rows[:].bitcast(I32)[:, :, COL_TOKEN], tables[:, 128:128 + n_tiles]))
                dve.memset(rows[:, :, COL_TOKEN + 1:], 0.0)
                dve.tensor_copy(place_i[:], place_r[:]).then_inc(r_place, 1)

                def prepare(s):
                    dve.wait_ge(f_r[s % NR], 16 * (s // NR + 1))
                    row = r_ring[:, s % NR, :]
                    dve.tensor_scalar(zz[:, s % 2, :], row[:, 0:d_model], row[:, COL_S1:COL_S1 + 1],
                                      row[:, COL_T1:COL_T1 + 1], ALU.mult, ALU.add).then_inc(f_base, 1)
                    dve.wait_ge(f_base, 2 * s + 1)
                    if s >= 2:
                        dve.wait_ge(f_t, s - 1)
                    dve.tensor_scalar(xhat[:, s % 2, :], zz[:, s % 2, :], row[:, COL_S2:COL_S2 + 1],
                                      row[:, COL_T2:COL_T2 + 1], ALU.mult, ALU.add).then_inc(f_xh, 1)
                    dve.tensor_tensor(base[:, s % NR, :], row[:, 0:d_model], zz[:, s % 2, :], ALU.add).then_inc(f_base, 1)

                def relu(s):
                    dve.wait_ge(f_h, 2 * s + 2)
                    if s >= 2:
                        dve.wait_ge(f_y, s - 1)
                    b1 = w_ring[:, s % NW, VEC + 2 * KC:]
                    for f in range(FC // 2, FC):
                        last = dve.tensor_scalar(hid_t[:, s % 2, f, :], hid_out(s, 1)[:, (f - 4) * P:(f - 3) * P],
                                                 b1[:, f:f + 1], 0.0, ALU.add, ALU.max)
                    last.then_inc(f_hd, 1)

                def finish(s):
                    dve.wait_ge(f_y, s + 1)
                    then_next(dve.tensor_tensor(upd[:, s % 2, :], upd_out(s), b2_ring[:, s % NW, :], ALU.add))
                    dve.wait_ge(f_base, 2 * s + 2)
                    if s >= NR:
                        dve.wait_ge(f_out[s % NR], 16 * (s // NR))
                    dve.scalar_tensor_tensor(out=fin[:, s % NR, :], in0=upd[:, s % 2, :],
                                             scalar=r_ring[:, s % NR, COL_ALPHA:COL_ALPHA + 1],
                                             in1=base[:, s % NR, :], op0=ALU.mult, op1=ALU.add).then_inc(f_o, 1)

                prepare(0)
                prepare(1)
                relu(0)
                for s in range(n_slots):
                    if s + 2 < n_slots:
                        prepare(s + 2)
                    if s + 1 < n_slots:
                        relu(s + 1)
                    finish(s)


def kernel(x, ctx_1024, L0_xattn_ln_m_g, L0_xattn_ln_m_b, L0_xattn_ln_l_g, L0_xattn_ln_l_b, L0_xattn_Wq, L0_xattn_Wkv,
           L0_xattn_Wout, L0_ffn_centroids, L0_ffn_ln_g, L0_ffn_ln_b, L0_ffn_w1, L0_ffn_b1, L0_ffn_w2, L0_ffn_b2):
    import numpy as np
    import concourse.bacc as bacc
    from concourse.bass_utils import run_bass_kernel_spmd

    p = 128
    n_batches, n_tok, d_model = x.shape
    n_experts, d_ff, _ = L0_ffn_w1.shape
    kc, fc = d_model // p, d_ff // p
    n_slots = n_batches + n_experts - 1

    def columns(v):
        v = np.asarray(v)
        return np.swapaxes(v.reshape(*v.shape[:-1], -1, p), -1, -2)

    ln_pack = np.stack([columns(v) for v in (L0_xattn_ln_m_g, L0_xattn_ln_m_b, L0_xattn_ln_l_g, L0_xattn_ln_l_b)], axis=1)
    centroids_t = np.asarray(L0_ffn_centroids).T.reshape(kc, p, n_experts).transpose(1, 0, 2)
    w1 = np.asarray(L0_ffn_w1).transpose(0, 2, 1).reshape(n_experts, kc, p, d_ff).transpose(0, 2, 1, 3)
    w2 = np.asarray(L0_ffn_w2).transpose(0, 2, 1).reshape(n_experts, fc, p, d_model).transpose(0, 2, 1, 3)
    experts = np.concatenate([w1.reshape(n_experts, p, -1), w2.reshape(n_experts, p, -1),
                              columns(L0_ffn_ln_g), columns(L0_ffn_ln_b), columns(L0_ffn_b1)], axis=2)

    consts = np.zeros((p, 3 * p + 160 + 64), np.float32)
    consts[:, 0:p] = np.eye(p)
    consts[:, p:2 * p] = np.triu(np.ones((p, p)), 1)
    consts[:, 2 * p:3 * p] = 1.0
    tables = consts[:, 3 * p:3 * p + 160]
    tables[:, 0:n_experts] = n_experts - np.arange(n_experts)
    tables[:, 32:32 + n_batches] = p * np.arange(n_batches)
    tables[:, 64:64 + n_slots] = np.arange(n_slots)
    tables[:, 128:128 + n_batches] = np.arange(n_batches)[None, :] * p + np.arange(p)[:, None]
    consts[:, 3 * p + 160:] = np.tril(np.ones((n_experts, n_experts)), -1).reshape(-1)

    arrays = {"x": x, "ctx_in": ctx_1024, "ln_pack": ln_pack, "w_q": L0_xattn_Wq, "w_kv": L0_xattn_Wkv,
              "w_out": L0_xattn_Wout, "centroids_t": centroids_t, "consts": consts, "experts": experts, "b2": L0_ffn_b2}
    arrays = {f"in_{k}": np.ascontiguousarray(v) for k, v in arrays.items()}
    nc = bacc.Bacc("TRN2", target_bir_lowering=False, num_devices=1)
    args = [nc.dram_tensor(k, v.shape, mybir.dt.from_np(v.dtype), kind="ExternalInput").ap() for k, v in arrays.items()]
    out = nc.dram_tensor("out", (n_batches * n_tok, d_model), F32, kind="ExternalOutput").ap()
    build(nc, *args, out)
    r = run_bass_kernel_spmd(nc, [arrays], core_ids=[0])
    return r.results[0]["out"].reshape(n_batches, n_tok, d_model)
```

```python
from contextlib import ExitStack

import concourse.bass as bass
from concourse import mybir

F32 = mybir.dt.float32
F32R = mybir.dt.float32r
I32 = mybir.dt.int32
ACT = mybir.ActivationFunctionType
ALU = mybir.AluOpType
AXIS_X = mybir.AxisListType.X

P = 128
DH = 64
EPS = 1e-5
BANK = 512
OUT_OF_RANGE = 1 << 20

BLOCK = 2 * P

COL_S1, COL_T1, COL_S2, COL_T2, COL_ALPHA, COL_TOKEN = range(256, 262)
ROW = 264

TAB_RANK, TAB_REGION, TAB_BLOCK, TAB_SLOT, TAB_TOKEN, N_TABLE = 0, 16, 32, 64, 96, 128

PASSES = ((0, 0), (0, 1), (1, 0))


def plan_jobs(n_batches):
    before = [("ln", 0, 0), ("ln", 1, 0)]
    before += [("q", 0, m) for m in range(4)] + [("k", 0, m) for m in range(4)] + [("v", 0, m) for m in range(4)]
    beside = []
    for b in range(n_batches):
        work = []
        if b + 1 < n_batches:
            work += [("k", b + 1, m) for m in range(4)] + [("v", b + 1, m) for m in range(4)]
        for s in range(4):
            if b % 2 == 1:
                part = work[(0, 3, 4, 6)[s]:(3, 4, 6, 8)[s]]
                if b + 1 < n_batches and s >= 1:
                    part = [("q", (b + 1) // 2, s - 1)] + part
            else:
                part = work[2 * s:2 * s + 2]
                if b >= 2 and s == 0:
                    part = [("q", b // 2, 3)] + part
                if b + 2 < n_batches and s >= 2:
                    part = part[:1] + [("ln", b + s, 0)] + part[1:]
            kind, of = (("aff", b - 2), ("rank", b - 2), ("wout", b - 1), ("zt", b - 1))[s]
            if of >= 0:
                at = (1, 0, 1, 1)[s]
                part = part[:at] + [(kind, of, 0)] + part[at:]
            beside.append(part)
    beside += [[("aff", n_batches - 2, 0)], [("rank", n_batches - 2, 0)]]
    after = [("wout", n_batches - 1, 0), ("zt", n_batches - 1, 0), ("aff", n_batches - 1, 0), ("rank", n_batches - 1, 0)]
    return before, beside, after


def build(nc, x, ctx_in, ln_pack, w_q, w_kv, w_out, centroids_t, consts, experts, b2, out):
    n_batches, _, d_model = x.shape
    inner = w_q.shape[1]
    n_experts = centroids_t.shape[2]

    d_ff = (experts.shape[2] - 12) // 4
    KC = d_model // P
    HC = inner // P
    FC = d_ff // P
    n_tiles = n_batches
    n_tokens = n_tiles * P
    n_slots = n_tokens // BLOCK + n_experts - 1
    spare = n_experts - 1
    region = n_tokens + BLOCK
    n_quads = n_batches * 4
    before, beside, after = plan_jobs(n_batches)
    all_jobs = before + [j for part in beside for j in part] + after
    number = {job: i for i, job in enumerate(all_jobs)}
    half_number = {}
    for job in all_jobs:
        if job[0] in "qk":
            half_number[job] = max(half_number.values(), default=0) + (1 if job[0] == "q" else 2)

    sorted_rows = nc.dram_tensor("sorted_rows", [n_experts * region + spare * BLOCK, ROW], F32, kind="Internal").ap()

    with ExitStack() as top:
        def sem(name):
            return top.enter_context(nc.semaphore(name))

        def sbuf(scope, name, shape, dtype=F32):
            return scope.enter_context(nc.sbuf_tensor(name, shape, dtype))

        psum = top.enter_context(nc.psum_tensor("psum", [P, 8, BANK], F32))
        ident = sbuf(top, "ident", [P, P])
        lower_ones = sbuf(top, "lower_ones", [P, 2, P])
        tables = sbuf(top, "tables", [P, N_TABLE])
        prefix = sbuf(top, "prefix", [P, n_experts, n_experts])
        onehot = sbuf(top, "onehot", [P, 2, n_experts])
        counts = sbuf(top, "counts", [P, 2, n_experts])
        best = sbuf(top, "best", [P, 2])
        filler = sbuf(top, "filler", [P, ROW])

        with ExitStack() as a:
            w_split = [sbuf(a, f"w_{h}", [P, KC, 3 * inner], F32R) for h in ("hi", "lo")]
            kv_t = [sbuf(a, f"kv_t_{h}", [P, KC, 4, 2 * P], F32R) for h in ("hi", "lo")]
            w_o = [sbuf(a, f"w_o_{h}", [P, HC, d_model], F32R) for h in ("hi", "lo")]
            q_t = [sbuf(a, f"q_t_{h}", [P, HC, 2 * P], F32R) for h in ("hi", "lo")]
            q_twice = sbuf(a, "q_twice", [P, 2 * HC, 2 * P], F32R)
            k_both = sbuf(a, "k_both", [P, 2, 2 * HC, 2 * P], F32R)
            v_n = sbuf(a, "v_n", [P, 2, 2, inner])
            y_t = sbuf(a, "y_t", [P, KC, 2, P])
            NPROB = 4
            prob = sbuf(a, "prob", [P, NPROB, 2, 2 * P])
            NPT = 4
            prob_t = sbuf(a, "prob_t", [P, NPT, 2, 2, P])
            head_out = [sbuf(a, f"head_out_{h}", [P, HC, P], F32R) for h in ("hi", "lo")]
            NROW = 3
            row_ring = sbuf(a, "row_ring", [P, NROW, ROW])
            place = sbuf(a, "place", [P, 2, n_experts])
            place_f = sbuf(a, "place_f", [P, 1])
            place_i = sbuf(a, "place_i", [P, NROW], I32)
            gate = sbuf(a, "gate", [P, 2, 2])
            NX, NCTX = 6, 2
            x_in = sbuf(a, "x_in", [P, NX, d_model])
            c_in = sbuf(a, "c_in", [P, NCTX, d_model])
            normed = sbuf(a, "normed", [P, 4, d_model])
            z_buf = sbuf(a, "z_buf", [P, d_model])
            z_t = sbuf(a, "z_t", [P, KC, P])
            cent = sbuf(a, "cent", [P, KC, n_experts])
            ln_w = sbuf(a, "ln_w", [P, 4, KC])
            stats = sbuf(a, "stats", [P, 4, 6])
            mean_var = sbuf(a, "mean_var", [P, 4, 2])
            ln_scale = sbuf(a, "ln_scale", [P, 2, 4])
            ln_shift = sbuf(a, "ln_shift", [P, 2, 4])
            tmp_v = sbuf(a, "tmp_v", [P, 4])
            var_eps = sbuf(a, "var_eps", [P, 4])
            minus_half = sbuf(a, "minus_half", [P, 4])
            neg_max = sbuf(a, "neg_max", [P, 8, 2])
            prob_sum = sbuf(a, "prob_sum", [P, 8, 2])
            inv_sum = sbuf(a, "inv_sum", [P, 8, 2])
            stats_z = sbuf(a, "stats_z", [P, 2, 6])
            mv_z = sbuf(a, "mv_z", [P, 2, 2])
            aff = sbuf(a, "aff", [P, 2, n_experts])
            rank_w = sbuf(a, "rank_w", [P, n_experts])
            rank_m = sbuf(a, "rank_m", [P, 1])

            s_const = sem("s_const")
            s_in = [sem("s_in0"), sem("s_in1")]
            s_w = [sem(f"s_w{i}") for i in range(3)]
            s_wo = sem("s_wo")
            s_whi = sem("s_whi")
            s_wlo = sem("s_wlo")
            s_lnp = sem("s_lnp")
            s_mv = sem("s_mv")
            s_mv1 = sem("s_mv1")
            s_mv2 = sem("s_mv2")
            s_st1 = sem("s_st1")
            s_st2 = sem("s_st2")
            s_pool = sem("s_pool")
            s_nrm = sem("s_nrm")
            s_job = sem("s_job")
            s_bank = [sem("s_bank0"), sem("s_bank1")]
            s_hi = sem("s_hi")
            s_lo = sem("s_lo")
            s_score = sem("s_score")
            s_max = sem("s_max")
            s_exp = sem("s_exp")
            s_inv = sem("s_inv")
            s_soft = sem("s_soft")
            s_tr = sem("s_tr")
            s_pt = sem("s_pt")
            s_pv = sem("s_pv")
            s_hoh = sem("s_hoh")
            s_ho = sem("s_ho")
            s_twice = [sem(f"s_twice{m}") for m in range(4)]
            s_half = sem("s_half")
            s_oh = sem("s_oh")
            s_gate = sem("s_gate")
            s_pos = sem("s_pos")
            s_scat = [sem(f"s_scat{i}") for i in range(NROW)]
            s_z = sem("s_z")
            s_dve = sem("s_dve")
            s_fill = sem("s_fill")
            s_pad = sem("s_pad")
            w_raw = [v_n[:, 0].rearrange("p s n -> p (s n)"), v_n[:, 1].rearrange("p s n -> p (s n)"),
                     prob[:].rearrange("p n i j -> p (n i j)")[:, 0:KC * inner]]
            w_raw = [w.rearrange("p (c n) -> p c n", c=KC) for w in w_raw]
            w_o_raw = prob_t[:].rearrange("p n i s t -> p (n i s t)")[:, 0:HC * d_model]

            block = a.enter_context(nc.Block())

            def unit_bank(n):
                return n % 3

            def tr_bank(n):
                return 3 + n % 2

            OUT_BANK = 5

            def job_bank(j):
                return psum[:, 6 + j % 2, :]

            def wait_read(eng, job):
                j = number[job]
                eng.wait_ge(s_bank[j % 2], j // 2 + 1)

            def wait_job(eng, job):
                eng.wait_ge(s_job, number[job] + 1)

            def unit_heads(n):
                quad, parity = n // 2, n % 2
                h0 = 4 * (quad % 4) + parity
                return quad // 4, (h0, h0 + 2)

            @block.sync
            def _(sp):
                def load_pair(g):
                    if g >= 1:
                        sp.wait_ge(s_nrm, g)
                    if g >= 3:
                        sp.wait_ge(s_z, 2 * (g - 3) + 2)
                    b = 2 * g
                    sp.dma_start(x_in[:, b % NX:b % NX + 2, :],
                                 x[b:b + 2].rearrange("b p d -> p b d")).then_inc(s_in[g % 2], 16)
                    sp.dma_start(c_in[:, b % NCTX:b % NCTX + 2, :],
                                 ctx_in[b:b + 2].rearrange("b p d -> p b d")).then_inc(s_in[g % 2], 16)

                load_pair(0)
                sp.dma_start(ident[:], consts[:, 0:P]).then_inc(s_const, 16)
                sp.dma_start(ln_w[:], ln_pack).then_inc(s_const, 16)
                for i, src in enumerate((w_q, w_kv[:, 0:inner], w_kv[:, inner:2 * inner])):
                    sp.dma_start(w_raw[i],
                                 src.rearrange("(c p) n -> p c n", p=P)).then_inc(s_w[i], 16)
                sp.dma_start(w_o_raw.rearrange("p (c n) -> p c n", c=HC), w_out.rearrange("(c p) n -> p c n", p=P)).then_inc(s_wo, 16)
                sp.dma_start(lower_ones[:], consts[:, P:3 * P].rearrange("p (a b) -> p a b", a=2)).then_inc(s_const, 16)
                sp.dma_start(tables[:], consts[:, 3 * P:3 * P + N_TABLE]).then_inc(s_const, 16)
                sp.dma_start(prefix[:], consts[:, 3 * P + N_TABLE:].rearrange("p (a b) -> p a b", a=n_experts)).then_inc(s_const, 16)
                sp.dma_start(cent[:], centroids_t).then_inc(s_const, 16)
                sp.wait_ge(s_pad, 2)
                sp.dma_start(sorted_rows[n_experts * region:, :].rearrange("(s p) c -> p s c", p=P),
                             filler[:, None, :].to_broadcast([P, spare * BLOCK // P, ROW])).then_inc(s_fill, 16)
                def repeat_queries(g):
                    for m in range(4):
                        sp.wait_ge(s_half, half_number[("q", g, m)])
                        if g >= 1:
                            sp.wait_ge(s_score, 2 * (8 * g - 4 + m) + 2)
                        for parity in range(2):
                            for dst_lo in (0, DH):
                                sp.dma_start(q_twice.bitcast(F32)[dst_lo:dst_lo + DH, 4 * m + parity:4 * m + 4:2, :],
                                             q_t[0].bitcast(F32)[parity * DH:(parity + 1) * DH, 2 * m:2 * m + 2, :]
                                             ).then_inc(s_twice[m], 16)

                for g in range(n_batches // 2):
                    if g + 1 < n_batches // 2:
                        load_pair(g + 1)
                    repeat_queries(g)
                for m in range(4):
                    sp.wait_ge(s_twice[m], 64 * (n_batches // 2))
                sp.wait_ge(s_fill, 16)

            @block.tensor
            def _(pe):
                def run_job(job):
                    kind, b, m = job
                    j = number[job]
                    bank = job_bank(j)
                    if j >= 2:
                        pe.wait_ge(s_bank[j % 2], j // 2)
                    if kind == "ln":
                        pe.wait_ge(s_nrm, b // 2 + 1)
                        for c in range(KC):
                            for side in range(2):
                                last = pe.transpose(bank[:, (2 * c + side) * P:(2 * c + side + 1) * P],
                                                    normed[:, 2 * side + b % 2, c * P:(c + 1) * P], ident[:])
                    elif kind in "qk":
                        first_b = 2 * b if kind == "q" else b
                        pe.wait_ge(s_hi, (2 * b + 2) if kind == "q" else b + 1)
                        pe.wait_ge(s_lo, (2 * b + 2) if kind == "q" else b + 1)
                        slot = first_b % 4
                        for cc in range(2):
                            col = (inner if kind == "k" else 0) + (2 * m + cc) * P
                            for i, (hw, hx) in enumerate(PASSES):
                                for c in range(KC):
                                    tokens = (kv_t[hx][:, c, slot, :] if kind == "k" else
                                              kv_t[hx][:, c, slot:slot + 2, P:2 * P])
                                    dst = bank[:, cc * 2 * P:(cc + 1) * 2 * P]
                                    if kind == "q":
                                        dst = dst.rearrange("p (a t) -> p a t", a=2)
                                    last = pe.matmul(dst, w_split[hw][:, c, col:col + P], tokens,
                                                     start=(i == 0 and c == 0), stop=(i == 2 and c == KC - 1))
                    elif kind == "v":
                        side, half = m // 2, m % 2
                        slot = b % 4
                        for i, (hx, hw) in enumerate(PASSES):
                            for c in range(KC):
                                last = pe.matmul(bank, kv_t[hx][:, c, slot, side * P:(side + 1) * P],
                                                 w_split[hw][:, c, 2 * inner + half * BANK:2 * inner + (half + 1) * BANK],
                                                 start=(i == 0 and c == 0), stop=(i == 2 and c == KC - 1))
                    elif kind == "wout":
                        pe.wait_ge(s_ho, 2 * b + 2)
                        for i, (ho, hw) in enumerate(PASSES):
                            for c in range(HC):
                                last = pe.matmul(bank[:, 0:d_model], head_out[ho][:, c, :], w_o[hw][:, c, :],
                                                 start=(i == 0 and c == 0), stop=(i == 2 and c == HC - 1))
                    elif kind == "zt":
                        pe.wait_ge(s_z, b + 1)
                        for c in range(KC):
                            last = pe.transpose(bank[:, c * P:(c + 1) * P], z_buf[:, c * P:(c + 1) * P], ident[:])
                    elif kind == "rank":
                        pe.wait_ge(s_oh, b + 1)
                        pe.matmul(bank[:, 0:n_experts], lower_ones[:, 0, :], onehot[:, b % 2, :], start=True, stop=False)
                        last = pe.matmul(bank[:, 0:n_experts], lower_ones[:, 1, :], counts[:, b % 2, :], start=False, stop=True)
                    else:
                        wait_read(pe, ("zt", b, 0))
                        for c in range(KC):
                            last = pe.matmul(bank[:, 0:n_experts], z_t[:, c, :], cent[:, c, :],
                                             start=(c == 0), stop=(c == KC - 1))
                    last.then_inc(s_job, 1)

                def scores(quad):
                    b = quad // 4
                    if quad % 4 == 0:
                        wait_read(pe, ("k", b, 3))
                        wait_read(pe, ("k", b, 2))
                    m = quad % 4
                    if b % 2 == 0:
                        wait_read(pe, ("q", b // 2, m))
                        pe.wait_ge(s_twice[m], 64 * (b // 2 + 1))
                    for n in (2 * quad, 2 * quad + 1):
                        if n >= 3:
                            pe.wait_ge(s_exp, 2 * (n - 3) + 2)
                    tokens = slice((b % 2) * P, (b % 2 + 1) * P)
                    for i in range(2):
                        for n in (2 * quad, 2 * quad + 1):
                            h = unit_heads(n)[1][i]
                            pe.matmul(psum[:, unit_bank(n), i * 2 * P:(i + 1) * 2 * P],
                                      q_twice[:, h, tokens], k_both[:, b % 2, h, :], start=True, stop=False)
                        for n in (2 * quad, 2 * quad + 1):
                            h = unit_heads(n)[1][i]
                            lo = DH * (h % 2)
                            ins = pe.matmul(psum[:, unit_bank(n), i * 2 * P:(i + 1) * 2 * P],
                                            q_t[1][lo:lo + DH, h // 2, tokens],
                                            k_both[lo:lo + DH, b % 2, h, :], start=False, stop=True)
                            if i == 1:
                                ins.then_inc(s_score, 1)

                def transposes(n):
                    pe.wait_ge(s_soft, n + 1)
                    if n >= 2:
                        pe.wait_ge(s_pt, n - 1)
                    for i in range(2):
                        for side in range(2):
                            last = pe.transpose(psum[:, tr_bank(n), (2 * i + side) * P:(2 * i + side + 1) * P],
                                                prob[:, n % NPROB, i, side * P:(side + 1) * P], ident[:])
                    last.then_inc(s_tr, 1)

                def outputs(quad):
                    b = quad // 4
                    if quad % 4 == 0:
                        wait_read(pe, ("v", b, 3))
                        wait_read(pe, ("v", b, 2))
                    pe.wait_ge(s_pt, 2 * quad + 2)
                    if quad % 2 == 0 and quad >= 2:
                        pe.wait_ge(s_ho, quad // 2)
                    for i in range(2):
                        for side in range(2):
                            for n in (2 * quad, 2 * quad + 1):
                                h = unit_heads(n)[1][i]
                                lo = DH * (h % 2)
                                slot = (h // 2) % 4
                                last = pe.matmul(psum[lo:lo + DH, OUT_BANK, slot * P:(slot + 1) * P],
                                                 v_n[:, b % 2, side, h * DH:(h + 1) * DH],
                                                 prob_t[:, n % NPT, i, side, :],
                                                 start=(side == 0), stop=(side == 1))
                    last.then_inc(s_pv, 1)

                pe.wait_ge(s_const, 6 * 16)
                for job in before[:2]:
                    run_job(job)
                pe.wait_ge(s_whi, 3 * KC * 2 + 2)
                pe.wait_ge(s_wlo, 3 * KC)
                for job in before[2:]:
                    run_job(job)
                for t in range(n_quads + 2):
                    jobs = beside[t]
                    if t < n_quads:
                        scores(t)
                    for job in jobs[:1]:
                        run_job(job)
                    if t >= 2:
                        outputs(t - 2)
                    for job in jobs[1:2]:
                        run_job(job)
                    if 1 <= t <= n_quads:
                        transposes(2 * t - 2)
                        transposes(2 * t - 1)
                    for job in jobs[2:]:
                        run_job(job)
                for job in after:
                    run_job(job)

            @block.scalar
            def _(act):
                def normalise(g):
                    act.wait_ge(s_lnp, g + 1)
                    if g >= 1:
                        wait_job(act, ("ln", 2 * g - 1, 0))
                    for j in range(4):
                        side, b = j // 2, 2 * g + j % 2
                        src = c_in[:, b % NCTX, :] if side == 0 else x_in[:, b % NX, :]
                        last = act.activation(normed[:, j, :], src, ACT.Identity,
                                              bias=ln_shift[:, g % 2, j:j + 1], scale=ln_scale[:, g % 2, j:j + 1])
                    last.then_inc(s_nrm, 1)

                def read_job(job):
                    kind, b, m = job
                    if kind not in ("ln", "q", "k", "v"):
                        return
                    j = number[job]
                    bank = job_bank(j)
                    wait_job(act, job)
                    if kind == "ln":
                        if b >= 1:
                            act.wait_ge(s_lo, b)
                        for c in range(KC):
                            for side in range(2):
                                last = act.activation(y_t[:, c, side, :],
                                                      bank[:, (2 * c + side) * P:(2 * c + side + 1) * P], ACT.Identity,
                                                      bias=ln_w[:, 2 * side + 1, c:c + 1], scale=ln_w[:, 2 * side, c:c + 1])
                    elif kind == "q":
                        if b >= 1:
                            act.wait_ge(s_twice[m], 64 * b)
                        last = act.activation(q_t[0][:, 2 * m:2 * m + 2, :].rearrange("p c t -> p (c t)"), bank,
                                              ACT.Copy, scale=DH ** -0.5)
                    elif kind == "k":
                        if b >= 2:
                            act.wait_ge(s_score, 8 * (b - 1))
                        for parity in range(2):
                            rows = slice(parity * DH, (parity + 1) * DH)
                            last = act.activation(k_both[rows, b % 2, 4 * m + parity:4 * m + 4:2, :],
                                                  bank[rows, :].rearrange("p (c t) -> p c t", c=2), ACT.Copy)
                            if parity == 0:
                                last.then_inc(s_half, 1)
                    else:
                        if b >= 2:
                            act.wait_ge(s_pv, 4 * (b - 1))
                        last = act.activation(v_n[:, b % 2, m // 2, (m % 2) * BANK:(m % 2 + 1) * BANK], bank, ACT.Copy)
                    last.then_inc(s_half if kind in "qk" else s_bank[j % 2], 1)

                def exponentials(n):
                    act.wait_ge(s_max, n + 1)
                    if n >= NPROB:
                        act.wait_ge(s_tr, n - NPROB + 1)
                    for i in range(2):
                        act.activation(prob[:, n % NPROB, i, :], psum[:, unit_bank(n), i * 2 * P:(i + 1) * 2 * P], ACT.Exp,
                                       bias=neg_max[:, n % 8, i:i + 1],
                                       accum_out=prob_sum[:, n % 8, i:i + 1]).then_inc(s_exp, 1)

                def copy_outputs(half):
                    act.wait_ge(s_pv, 2 * half + 2)
                    b = half // 2
                    if b >= 1 and half % 2 == 0:
                        wait_job(act, ("wout", b - 1, 0))
                    act.activation(head_out[0][:, 4 * (half % 2):4 * (half % 2) + 4, :].rearrange("p c t -> p (c t)"),
                                   psum[:, OUT_BANK, :], ACT.Copy).then_inc(s_hoh, 1)

                def norm_x1(b):
                    act.wait_ge(s_st1, b + 1)
                    if b >= 1:
                        wait_job(act, ("zt", b - 1, 0))
                        act.wait_ge(s_mv2, b)
                    row = row_ring[:, b % NROW, :]
                    act.activation(z_buf[:], row[:, 0:d_model], ACT.Identity, bias=row[:, COL_T1:COL_T1 + 1],
                                   scale=row[:, COL_S1:COL_S1 + 1]).then_inc(s_z, 1)

                def gate_of(b):
                    act.wait_ge(s_oh, b + 1)
                    if b >= 2:
                        act.wait_ge(s_pos, b - 1)
                    act.activation(gate[:, 0, b % 2:b % 2 + 1], best[:, b % 2:b % 2 + 1], ACT.Exp, scale=-1.0).then_inc(s_gate, 1)

                act.wait_ge(s_const, 6 * 16)
                normalise(0)
                for job in before:
                    read_job(job)
                for t in range(n_quads + 2):
                    jobs = beside[t]
                    for kind, b, _ in jobs:
                        if kind == "rank":
                            gate_of(b)
                    if t < n_quads:
                        exponentials(2 * t)
                    for job in jobs[:1]:
                        read_job(job)
                    if t < n_quads:
                        exponentials(2 * t + 1)
                    for job in jobs[1:2]:
                        read_job(job)
                    if t >= 3 and t % 2 == 1:
                        copy_outputs((t - 3) // 2)
                    for job in jobs[2:]:
                        read_job(job)
                    for kind, b, _ in jobs:
                        if kind == "wout":
                            norm_x1(b)
                    b = t // 4
                    if t % 8 == 1 and b + 2 < n_batches:
                        normalise(b // 2 + 1)
                norm_x1(n_batches - 1)
                gate_of(n_batches - 1)

            @block.vector
            def _(dve):
                chained = [0]

                def then_next(ins):
                    chained[0] += 1
                    ins.then_inc(s_dve, 1)
                    dve.wait_ge(s_dve, chained[0])

                def layer_norm_stats(g, j):
                    if j == 0:
                        dve.wait_ge(s_in[g % 2], 32 * (g // 2 + 1))
                        if g >= 1:
                            dve.wait_ge(s_lnp, g)
                    side, b = j // 2, 2 * g + j % 2
                    src = c_in[:, b % NCTX, :] if side == 0 else x_in[:, b % NX, :]
                    then_next(dve.bn_stats(stats[:, j, :], src))
                    dve.bn_aggr(mean_var[:, j, :], stats[:, j, :]).then_inc(s_mv, 1)

                def maxima(n):
                    dve.wait_ge(s_score, n + 1)
                    dve.tensor_reduce(neg_max[:, n % 8, :], psum[:, unit_bank(n), :].rearrange("p (i j) -> p i j", i=2),
                                      AXIS_X, ALU.max, negate=True).then_inc(s_max, 1)

                def inverse_sums(n):
                    dve.wait_ge(s_exp, 2 * n + 2)
                    dve.reciprocal(inv_sum[:, n % 8, :], prob_sum[:, n % 8, :]).then_inc(s_inv, 1)

                def copy_transposed(n):
                    dve.wait_ge(s_tr, n + 1)
                    if n >= NPT:
                        dve.wait_ge(s_pv, (n - NPT) // 2 + 1)
                    dve.tensor_copy(prob_t[:, n % NPT].rearrange("p i s t -> p (i s t)"), psum[:, tr_bank(n), :]).then_inc(s_pt, 1)

                def read_job(job):
                    kind, b, m = job
                    j = number[job]
                    bank = job_bank(j)
                    if kind == "ln":
                        wait_read(dve, job)
                        if b >= 4:
                            wait_job(dve, ("v", b - 4, 3))
                            wait_job(dve, ("q", (b - 4) // 2, 3))
                        dve.tensor_copy(kv_t[0][:, :, b % 4, :].rearrange("p c (s t) -> p c s t", s=2), y_t[:]).then_inc(s_hi, 1)
                    elif kind in "qk":
                        if kind == "q":
                            dve.wait_ge(s_half, half_number[job])
                            if b >= 1:
                                dve.wait_ge(s_score, 2 * (8 * b - 4 + m) + 2)
                            hi, lo = [q[:, 2 * m:2 * m + 2, :].rearrange("p c t -> p (c t)") for q in q_t]
                            ins = dve.scalar_tensor_tensor(out=lo, in0=bank, scalar=DH ** -0.5, in1=hi,
                                                           op0=ALU.mult, op1=ALU.subtract)
                        else:
                            for parity in range(2):
                                dve.wait_ge(s_half, half_number[job] - 1 + parity)
                                heads = k_both[:, b % 2, 4 * m + parity:4 * m + 4:2, :]
                                hi, lo = slice(parity * DH, (parity + 1) * DH), slice((1 - parity) * DH, (2 - parity) * DH)
                                ins = dve.tensor_tensor(heads[lo], bank[hi, :].rearrange("p (c t) -> p c t", c=2), heads[hi],
                                                        ALU.subtract)
                        ins.then_inc(s_bank[j % 2], 1)
                    elif kind == "wout":
                        wait_job(dve, job)
                        if b >= NROW:
                            dve.wait_ge(s_scat[b % NROW], 16 * (b // NROW))
                        x1 = row_ring[:, b % NROW, 0:d_model]
                        ins = dve.tensor_tensor(x1, bank[:, 0:d_model], x_in[:, b % NX, :], ALU.add)
                        ins.then_inc(s_bank[j % 2], 1)
                        dve.wait_ge(s_bank[j % 2], j // 2 + 1)
                        then_next(dve.bn_stats(stats_z[:, 0, :], x1))
                        if b >= 1:
                            dve.wait_ge(s_st1, b)
                        dve.bn_aggr(mv_z[:, 0, :], stats_z[:, 0, :]).then_inc(s_mv1, 1)
                    elif kind == "zt":
                        wait_job(dve, job)
                        if b >= 1:
                            wait_job(dve, ("aff", b - 1, 0))
                        dve.tensor_copy(z_t[:].rearrange("p c t -> p (c t)"), bank[:, 0:KC * P]).then_inc(s_bank[j % 2], 1)
                        dve.wait_ge(s_z, b + 1)
                        then_next(dve.bn_stats(stats_z[:, 1, :], z_buf[:]))
                        if b >= 1:
                            dve.wait_ge(s_st2, b)
                        dve.bn_aggr(mv_z[:, 1, :], stats_z[:, 1, :]).then_inc(s_mv2, 1)
                    elif kind == "aff":
                        wait_job(dve, job)
                        if b >= 1:
                            wait_job(dve, ("rank", b - 1, 0))
                            dve.wait_ge(s_pos, b)
                        scores_b, same = aff[:, 0, :], aff[:, 1, :]
                        dve.tensor_copy(scores_b, bank[:, 0:n_experts]).then_inc(s_bank[j % 2], 1)
                        dve.wait_ge(s_bank[j % 2], j // 2 + 1)
                        then_next(dve.tensor_reduce(best[:, b % 2:b % 2 + 1], scores_b, AXIS_X, ALU.max))
                        then_next(dve.tensor_scalar(same, scores_b, best[:, b % 2:b % 2 + 1], None, ALU.is_equal))
                        then_next(dve.tensor_tensor(rank_w[:], same, tables[:, TAB_RANK:TAB_RANK + n_experts], ALU.mult))
                        then_next(dve.tensor_reduce(rank_m[:], rank_w[:], AXIS_X, ALU.max))
                        then_next(dve.tensor_scalar(onehot[:, b % 2, :], rank_w[:], rank_m[:, 0:1], None, ALU.is_equal))
                        dve.tensor_tensor(counts[:, (b + 1) % 2, :], counts[:, b % 2, :], onehot[:, b % 2, :], ALU.add).then_inc(s_oh, 1)
                        dve.wait_ge(s_oh, b + 1)
                    elif kind == "rank":
                        wait_job(dve, job)
                        row = row_ring[:, b % NROW, :]
                        dve.tensor_tensor(place[:, 0, :], bank[:, 0:n_experts], tables[:, TAB_REGION:TAB_REGION + n_experts],
                                          ALU.add).then_inc(s_bank[j % 2], 1)
                        dve.wait_ge(s_bank[j % 2], j // 2 + 1)
                        dve.tensor_copy(row.bitcast(I32)[:, COL_TOKEN:COL_TOKEN + 1], tables[:, TAB_TOKEN + b:TAB_TOKEN + b + 1])
                        then_next(dve.tensor_tensor(place[:, 1, :], place[:, 0, :], onehot[:, b % 2, :], ALU.mult))
                        dve.wait_ge(s_gate, b + 1)
                        dve.tensor_scalar(gate[:, 1, b % 2:b % 2 + 1], gate[:, 0, b % 2:b % 2 + 1], 1.0, None, ALU.add)
                        then_next(dve.tensor_reduce(place_f[:], place[:, 1, :], AXIS_X, ALU.add))
                        dve.reciprocal(row[:, COL_ALPHA:COL_ALPHA + 1], gate[:, 1, b % 2:b % 2 + 1])
                        dve.tensor_copy(place_i[:, b % NROW:b % NROW + 1], place_f[:]).then_inc(s_pos, 1)

                def low_outputs(half):
                    dve.wait_ge(s_hoh, half + 1)
                    part = slice(4 * (half % 2), 4 * (half % 2) + 4)
                    dve.tensor_tensor(head_out[1][:, part, :].rearrange("p c t -> p (c t)"), psum[:, OUT_BANK, :],
                                      head_out[0][:, part, :].rearrange("p c t -> p (c t)"), ALU.subtract).then_inc(s_ho, 1)

                dve.memset(row_ring[:, :, COL_TOKEN + 1:], 0.0)
                then_next(dve.memset(counts[:, 0, :], 0.0))
                for j in range(4):
                    layer_norm_stats(0, j)
                for i in range(3):
                    dve.wait_ge(s_w[i], 16)
                    for c in range(KC):
                        cols = slice(i * inner, (i + 1) * inner)
                        raw, hi, lo = w_raw[i][:, c, :], w_split[0][:, c, cols], w_split[1][:, c, cols]
                        dve.tensor_copy(hi, raw).then_inc(s_whi, 1)
                        dve.wait_ge(s_whi, 2 * (i * KC + c) + 1)
                        half = inner // 2
                        dve.tensor_tensor(lo[:, 0:half], raw[:, 0:half], hi[:, 0:half], ALU.subtract).then_inc(s_whi, 1)
                dve.wait_ge(s_wo, 16)
                flat = [w[:].rearrange("p c n -> p (c n)") for w in w_o]
                dve.tensor_copy(flat[0], w_o_raw).then_inc(s_whi, 1)
                dve.wait_ge(s_whi, 2 * 3 * KC + 1)
                dve.tensor_tensor(flat[1], w_o_raw, flat[0], ALU.subtract).then_inc(s_whi, 1)
                for job in before:
                    read_job(job)
                for j in range(4):
                    layer_norm_stats(1, j)
                dve.wait_ge(s_const, 6 * 16)
                for t in range(n_quads + 2):
                    jobs = beside[t]
                    if t < n_quads:
                        maxima(2 * t)
                        maxima(2 * t + 1)
                    for job in jobs[:1]:
                        read_job(job)
                    if t < n_quads:
                        inverse_sums(2 * t)
                        inverse_sums(2 * t + 1)
                    for job in jobs[1:2]:
                        read_job(job)
                    if t >= 3 and t % 2 == 1:
                        low_outputs((t - 3) // 2)
                    if 1 <= t <= n_quads:
                        copy_transposed(2 * t - 2)
                        copy_transposed(2 * t - 1)
                    for job in jobs[2:]:
                        read_job(job)
                    if t % 8 >= 4 and t // 8 + 2 < n_batches // 2:
                        layer_norm_stats(t // 8 + 2, t % 4)
                for job in after:
                    read_job(job)

            @block.gpsimd
            def _(pool):
                def low_half(b):
                    pool.wait_ge(s_hi, b + 1)
                    pool.tensor_tensor(kv_t[1][:, :, b % 4, :].rearrange("p c (s t) -> p c s t", s=2), y_t[:],
                                       kv_t[0][:, :, b % 4, :].rearrange("p c (s t) -> p c s t", s=2),
                                       ALU.subtract).then_inc(s_lo, 1)

                def soften(n):
                    pool.wait_ge(s_inv, n + 1)
                    probs = prob[:, n % NPROB]
                    pool.tensor_tensor(probs, probs, inv_sum[:, n % 8, :, None].to_broadcast([P, 2, 2 * P]),
                                       ALU.mult).then_inc(s_soft, 1)

                chained = [0]

                def then_next(ins):
                    chained[0] += 1
                    ins.then_inc(s_pool, 1)
                    pool.wait_ge(s_pool, chained[0])

                def inv_sqrt(dst, var):
                    n = var.shape[1]
                    then_next(pool.tensor_scalar(var_eps[:, 0:n], var, EPS, None, ALU.add))
                    return pool.tensor_tensor(dst, var_eps[:, 0:n], minus_half[:, 0:n], ALU.pow)

                def layer_norm_scales(g):
                    pool.wait_ge(s_mv, 4 * (g + 1))
                    if g >= 2:
                        pool.wait_ge(s_nrm, g - 1)
                    scale, shift = ln_scale[:, g % 2, :], ln_shift[:, g % 2, :]
                    mean, var = mean_var[:, :, 0], mean_var[:, :, 1]
                    then_next(inv_sqrt(scale, var))
                    then_next(pool.tensor_tensor(tmp_v[:, 0:2], var[:, 2:4], scale[:, 2:4], ALU.mult))
                    then_next(pool.tensor_tensor(tmp_v[:, 2:4], tmp_v[:, 0:2], scale[:, 2:4], ALU.mult))
                    then_next(inv_sqrt(tmp_v[:, 0:2], tmp_v[:, 2:4]))
                    then_next(pool.tensor_tensor(scale[:, 2:4], scale[:, 2:4], tmp_v[:, 0:2], ALU.mult))
                    then_next(pool.tensor_tensor(shift, mean, scale, ALU.mult))
                    pool.tensor_scalar(shift, shift, -1.0, None, ALU.mult).then_inc(s_lnp, 1)

                def row_scales(b, which, s_from, s_to):
                    pool.wait_ge(s_from, b + 1)
                    col = (COL_S1, COL_S2)[which]
                    row = row_ring[:, b % NROW, :]
                    scale, shift = row[:, col:col + 1], row[:, col + 1:col + 2]
                    then_next(inv_sqrt(scale, mv_z[:, which, 1:2]))
                    then_next(pool.tensor_tensor(shift, mv_z[:, which, 0:1], scale, ALU.mult))
                    pool.tensor_scalar(shift, shift, -1.0, None, ALU.mult).then_inc(s_to, 1)

                then_next(pool.memset(minus_half[:], -0.5))
                def scatter(b):
                    pool.wait_ge(s_pos, b + 1)
                    pool.wait_ge(s_st2, b + 1)
                    pool.indirect_dma_start(out=sorted_rows, out_offset=bass.IndirectOffsetOnAxis(
                        ap=place_i[:, b % NROW:b % NROW + 1], axis=0),
                        in_=row_ring[:, b % NROW, :], in_offset=None).then_inc(s_scat[b % NROW], 16)

                layer_norm_scales(0)
                pool.memset(filler[:], 0.0).then_inc(s_pad, 1)
                pool.wait_ge(s_pad, 1)
                pool.memset(filler[:].bitcast(I32)[:, COL_TOKEN:COL_TOKEN + 1], OUT_OF_RANGE).then_inc(s_pad, 1)
                low_half(0)
                low_half(1)
                for i in range(3):
                    for c in range(KC):
                        pool.wait_ge(s_whi, 2 * (i * KC + c) + 1)
                        cols = slice(i * inner + inner // 2, (i + 1) * inner)
                        pool.tensor_tensor(w_split[1][:, c, cols], w_raw[i][:, c, inner // 2:], w_split[0][:, c, cols],
                                           ALU.subtract).then_inc(s_wlo, 1)
                for t in range(n_quads + 2):
                    if t < n_quads:
                        soften(2 * t)
                        soften(2 * t + 1)
                    for job in beside[t - 1] if t else []:
                        if job[0] == "rank":
                            scatter(job[1])
                    for job in beside[t]:
                        if job[0] == "ln":
                            low_half(job[1])
                        if job[0] == "wout":
                            row_scales(job[1], 0, s_mv1, s_st1)
                        if job[0] == "zt":
                            row_scales(job[1], 1, s_mv2, s_st2)
                    if t == 0:
                        layer_norm_scales(1)
                    elif t % 8 == 7 and t // 8 + 2 < n_batches // 2:
                        layer_norm_scales(t // 8 + 2)
                scatter(n_batches - 2)
                row_scales(n_batches - 1, 0, s_mv1, s_st1)
                row_scales(n_batches - 1, 1, s_mv2, s_st2)
                scatter(n_batches - 1)
                for i in range(NROW):
                    pool.wait_ge(s_scat[i], 16 * len(range(i, n_batches, NROW)))

        with ExitStack() as bb:
            NW = 2
            NR = 4
            width = experts.shape[2]
            n_w = KC * d_ff
            w_ring = [sbuf(bb, f"w{y}_ring", [P, NW, n_w]) for y in (1, 2)]
            vec_ring = sbuf(bb, "vec_ring", [P, NR, width - 2 * n_w])
            b2_ring = sbuf(bb, "b2_ring", [P, NR, d_model])
            w_hl = [[sbuf(bb, f"w{y}_{h}", [P, NW, n_w], F32R) for h in ("hi", "lo")] for y in (1, 2)]
            r_ring = sbuf(bb, "r_ring", [P, NR, 2, ROW])
            zz = sbuf(bb, "zz", [P, 2, 2, d_model])
            xhat = sbuf(bb, "xhat", [P, 2, 2, d_model])
            base = sbuf(bb, "base", [P, NR, 2, d_model])
            xn = sbuf(bb, "xn", [P, KC, BLOCK])
            xn_hl = [sbuf(bb, f"xn_{h}", [P, 2, KC, BLOCK], F32R) for h in ("hi", "lo")]
            hid = sbuf(bb, "hid", [P, FC, BLOCK])
            hid_hl = [sbuf(bb, f"hid_{h}", [P, 2, FC, BLOCK], F32R) for h in ("hi", "lo")]
            upd = sbuf(bb, "upd", [P, 2, d_model])
            fin = sbuf(bb, "fin", [P, 2, 2, d_model])
            n_over = n_tokens // BLOCK
            over = sbuf(bb, "over", [P, n_experts, n_over])
            blocks_e = sbuf(bb, "blocks_e", [P, n_experts])
            pre = sbuf(bb, "pre", [P, n_experts, n_experts])
            ends = sbuf(bb, "ends", [P, n_experts])
            total_e = sbuf(bb, "total_e", [P, n_experts])
            tail_f = sbuf(bb, "tail_f", [P, n_experts])
            behind = sbuf(bb, "behind", [1, n_slots, n_experts])
            begun = sbuf(bb, "begun", [1, n_slots, n_experts])
            slot_e = sbuf(bb, "slot_e", [1, n_slots])
            slot_b = sbuf(bb, "slot_b", [1, n_slots])
            slot_k = sbuf(bb, "slot_k", [1, n_slots])
            slot_r = sbuf(bb, "slot_r", [1, 2, n_slots])
            slot_i = sbuf(bb, "slot_i", [1, 2, n_slots], I32)
            tail_i = sbuf(bb, "tail_i", [1, n_experts], I32)

            r_dve = sem("r_dve")
            r_mm = sem("r_mm")
            r_slot = sem("r_slot")
            r_tail = sem("r_tail")
            f_w = [[sem(f"f_w{y}_{i}") for i in range(NW)] for y in (1, 2)]
            f_v = [sem(f"f_v{i}") for i in range(NR)]
            f_r = [sem(f"f_r{i}") for i in range(NR)]
            f_wh = [sem("f_w1h"), sem("f_w2h")]
            f_wd = [sem("f_w1d"), sem("f_w2d")]
            f_wp = [sem("f_w1p"), sem("f_w2p")]
            f_z = sem("f_z")
            f_xh = sem("f_xh")
            f_base = sem("f_base")
            f_t = sem("f_t")
            f_xa = sem("f_xa")
            f_xd = sem("f_xd")
            f_h = sem("f_h")
            f_ha = sem("f_ha")
            f_hh = sem("f_hh")
            f_hl = sem("f_hl")
            f_y = sem("f_y")
            f_u = sem("f_u")
            f_o = sem("f_o")
            f_out = [sem(f"f_out{i}") for i in range(2)]

            block = bb.enter_context(nc.Block())
            TOTAL_BANK = 0
            POOL_COLS = n_w // 4

            def weights_used(eng, y, s):
                eng.wait_ge(*((f_h, FC // 2 * (s + 1)) if y == 0 else (f_y, 2 * (s + 1))))

            def tr_out(s):
                return psum[:, s % 2, :]

            def hid_out(i):
                return psum[:, 2 + i, :]

            def upd_out(s):
                return psum[:, 6 + s % 2, :]

            @block.sync
            def _(sp):
                def load_weights(y, s, e):
                    if s >= NW:
                        sp.wait_ge(f_wd[y], s - NW + 1)
                        sp.wait_ge(f_wp[y], s - NW + 1)
                    source = experts[bass.DynSlice(e, 1), :, y * n_w:(y + 1) * n_w].rearrange("o p n -> p (o n)")
                    sp.dma_start(w_ring[y][:, s % NW, :], source).then_inc(f_w[y][s % NW], 16)

                def load_vectors(s, e):
                    if s >= NR:
                        sp.wait_ge(f_o, 2 * (s - NR) + 2)
                        sp.wait_ge(f_out[(s - NR) % 2], 32 * ((s - NR) // 2 + 1))
                    source = experts[bass.DynSlice(e, 1), :, 2 * n_w:].rearrange("o p n -> p (o n)")
                    sp.dma_start(vec_ring[:, s % NR, :], source).then_inc(f_v[s % NR], 16)
                    sp.dma_start(b2_ring[:, s % NR, :], b2[bass.DynSlice(e, 1), :].to_broadcast([P, d_model])
                                 ).then_inc(f_v[s % NR], 16)

                def load_rows(s):
                    first = sp.value_load(slot_i[0:1, 1, s:s + 1], min_val=0, max_val=n_experts * region + (spare - 1) * BLOCK)
                    sp.dma_start(r_ring[:, s % NR, :, :], sorted_rows[bass.DynSlice(first, BLOCK), :]
                                 .rearrange("(a p) c -> p a c", p=P)).then_inc(f_r[s % NR], 16)

                def expert_of(s):
                    return sp.value_load(slot_i[0:1, 0, s:s + 1], min_val=0, max_val=n_experts - 1)

                sp.wait_ge(r_slot, 1)
                for e in range(n_experts):
                    first = sp.value_load(tail_i[0:1, e:e + 1], min_val=0, max_val=n_experts * region - BLOCK)
                    sp.dma_start(sorted_rows[bass.DynSlice(first, BLOCK), :].rearrange("(a p) c -> p a c", p=P),
                                 filler[:, None, :].to_broadcast([P, BLOCK // P, ROW])).then_inc(r_tail, 16)
                e = expert_of(0)
                load_weights(0, 0, e)
                load_vectors(0, e)
                sp.wait_ge(r_tail, 16 * n_experts)
                load_rows(0)
                load_weights(1, 0, e)
                for s in range(1, n_slots):
                    e = expert_of(s)
                    load_vectors(s, e)
                    load_rows(s)
                    load_weights(0, s, e)
                    load_weights(1, s, e)

            @block.gpsimd
            def _(pool):
                def low_weights(y, s):
                    pool.wait_ge(f_wh[y], s + 1)
                    if s >= NW:
                        weights_used(pool, y, s - NW)
                    part = slice(0, POOL_COLS)
                    pool.tensor_tensor(w_hl[y][1][:, s % NW, part], w_ring[y][:, s % NW, part], w_hl[y][0][:, s % NW, part],
                                       ALU.subtract).then_inc(f_wp[y], 1)

                def add_base(s):
                    pool.wait_ge(f_z, 2 * s + 2)
                    if s >= NR:
                        pool.wait_ge(f_o, 2 * (s - NR) + 2)
                    pool.tensor_tensor(base[:, s % NR], r_ring[:, s % NR, :, 0:d_model], zz[:, s % 2], ALU.add).then_inc(f_base, 1)

                def write_rows(s):
                    for i in range(2):
                        pool.wait_ge(f_o, 2 * s + i + 1)
                        pool.indirect_dma_start(out=out, out_offset=bass.IndirectOffsetOnAxis(
                            ap=r_ring[:, s % NR, i, COL_TOKEN:COL_TOKEN + 1].bitcast(I32), axis=0),
                            in_=fin[:, s % 2, i, :], in_offset=None,
                            bounds_check=n_tokens - 1, oob_is_err=False).then_inc(f_out[s % 2], 16)

                add_base(0)
                low_weights(0, 0)
                add_base(1)
                low_weights(0, 1)
                low_weights(1, 0)
                for s in range(n_slots):
                    if s + 2 < n_slots:
                        add_base(s + 2)
                        low_weights(0, s + 2)
                    if s + 1 < n_slots:
                        low_weights(1, s + 1)
                    write_rows(s)
                for i in range(2):
                    pool.wait_ge(f_out[i], 32 * len(range(i, n_slots, 2)))

            @block.tensor
            def _(pe):
                pe.matmul(psum[:, TOTAL_BANK, 0:n_experts], lower_ones[:, 1, :], counts[:, n_tiles % 2, :],
                          start=True, stop=True).then_inc(r_mm, 1)

                def transposes(s):
                    pe.wait_ge(f_xh, s + 1)
                    if s >= 2:
                        pe.wait_ge(f_xa, s - 1)
                    for c in range(KC):
                        for i in range(2):
                            last = pe.transpose(tr_out(s)[:, (2 * c + i) * P:(2 * c + i + 1) * P],
                                                xhat[:, s % 2, i, c * P:(c + 1) * P], ident[:])
                    last.then_inc(f_t, 1)

                def layer_1(s):
                    pe.wait_ge(f_xd, 2 * s + 2)
                    pe.wait_ge(f_wd[0], s + 1)
                    pe.wait_ge(f_wp[0], s + 1)
                    for f in range(FC):
                        if f % 2 == 0 and s >= 1:
                            pe.wait_ge(f_ha, FC * (s - 1) + f + 2)
                        dst = hid_out(f // 2)[:, (f % 2) * BLOCK:(f % 2 + 1) * BLOCK]
                        for i, (hw, hx) in enumerate(PASSES):
                            w1 = w_hl[0][hw][:, s % NW, :].rearrange("p (c f) -> p c f", c=KC)
                            for c in range(KC):
                                last = pe.matmul(dst, w1[:, c, f * P:(f + 1) * P], xn_hl[hx][:, s % 2, c, :],
                                                 start=(i == 0 and c == 0), stop=(i == 2 and c == KC - 1))
                        if f % 2 == 1:
                            last.then_inc(f_h, 1)

                def layer_2(s):
                    pe.wait_ge(f_wd[1], s + 1)
                    pe.wait_ge(f_wp[1], s + 1)
                    if s >= 2:
                        pe.wait_ge(f_u, 2 * (s - 2) + 2)
                    for i in range(2):
                        dst = upd_out(s)[:, i * d_model:(i + 1) * d_model]
                        for f in range(FC):
                            if f % 4 == 0 and i == 0:
                                pe.wait_ge(f_hl, 2 * s + f // 4 + 1)
                            for j, (hh, hw) in enumerate(PASSES):
                                w2 = w_hl[1][hw][:, s % NW, :].rearrange("p (f d) -> p f d", f=FC)
                                last = pe.matmul(dst, hid_hl[hh][:, s % 2, f, i * P:(i + 1) * P], w2[:, f, :],
                                                 start=(f == 0 and j == 0), stop=(f == FC - 1 and j == 2))
                        last.then_inc(f_y, 1)

                transposes(0)
                layer_1(0)
                transposes(1)
                for s in range(n_slots):
                    if s + 1 < n_slots:
                        layer_1(s + 1)
                    if s + 2 < n_slots:
                        transposes(s + 2)
                    layer_2(s)

            @block.scalar
            def _(act):
                def high_weights(y, s):
                    act.wait_ge(f_w[y][s % NW], 16 * (s // NW + 1))
                    if s >= NW:
                        weights_used(act, y, s - NW)
                    act.activation(w_hl[y][0][:, s % NW, :], w_ring[y][:, s % NW, :], ACT.Copy).then_inc(f_wh[y], 1)

                def z_of(s):
                    act.wait_ge(f_r[s % NR], 16 * (s // NR + 1))
                    if s >= 2:
                        act.wait_ge(f_xh, s - 1)
                        act.wait_ge(f_base, s - 1)
                    for i in range(2):
                        row = r_ring[:, s % NR, i, :]
                        act.activation(zz[:, s % 2, i, :], row[:, 0:d_model], ACT.Identity, bias=row[:, COL_T1:COL_T1 + 1],
                                       scale=row[:, COL_S1:COL_S1 + 1]).then_inc(f_z, 1)

                def gain_bias(s):
                    act.wait_ge(f_t, s + 1)
                    act.wait_ge(f_v[s % NR], 32 * (s // NR + 1))
                    if s >= 1:
                        act.wait_ge(f_xd, 2 * s)
                    vec = vec_ring[:, s % NR, 0:2 * KC]
                    for c in range(KC):
                        last = act.activation(xn[:, c, :], tr_out(s)[:, c * BLOCK:(c + 1) * BLOCK], ACT.Identity,
                                              bias=vec[:, KC + c:KC + c + 1], scale=vec[:, c:c + 1])
                    last.then_inc(f_xa, 1)

                def relu(s):
                    b1 = vec_ring[:, s % NR, 2 * KC:]
                    for f in range(FC):
                        if f % 2 == 0:
                            act.wait_ge(f_h, FC // 2 * s + f // 2 + 1)
                        if s >= 1 and f % 4 == 0:
                            act.wait_ge(f_hl, 2 * (s - 1) + f // 4 + 1)
                        act.activation(hid[:, f, :], hid_out(f // 2)[:, (f % 2) * BLOCK:(f % 2 + 1) * BLOCK], ACT.Relu,
                                       bias=b1[:, f:f + 1]).then_inc(f_ha, 1)

                high_weights(0, 0)
                z_of(0)
                gain_bias(0)
                z_of(1)
                high_weights(0, 1)
                relu(0)
                gain_bias(1)
                high_weights(1, 0)
                for s in range(n_slots):
                    if s + 2 < n_slots:
                        z_of(s + 2)
                        high_weights(0, s + 2)
                    if s + 1 < n_slots:
                        relu(s + 1)
                    if s + 2 < n_slots:
                        gain_bias(s + 2)
                    if s + 1 < n_slots:
                        high_weights(1, s + 1)

            @block.vector
            def _(dve):
                chained = [0]

                def then_next(ins):
                    chained[0] += 1
                    ins.then_inc(r_dve, 1)
                    dve.wait_ge(r_dve, chained[0])

                slots = [1, n_slots, n_experts]
                dve.wait_ge(r_mm, 1)
                then_next(dve.tensor_copy(total_e[:], psum[:, TOTAL_BANK, 0:n_experts]))
                then_next(dve.tensor_tensor(tail_f[:], total_e[:], tables[:, TAB_REGION:TAB_REGION + n_experts], ALU.add))
                dve.tensor_copy(tail_i[:], tail_f[0:1, :])
                then_next(dve.tensor_tensor(over[:], total_e[:, :, None].to_broadcast([P, n_experts, n_over]),
                                            tables[:, None, TAB_BLOCK:TAB_BLOCK + n_over].to_broadcast([P, n_experts, n_over]),
                                            ALU.is_gt))
                then_next(dve.tensor_reduce(blocks_e[:], over[:], AXIS_X, ALU.add))
                then_next(dve.tensor_tensor(pre[:], prefix[:], blocks_e[:, None, :].to_broadcast([P, n_experts, n_experts]), ALU.mult))
                then_next(dve.tensor_reduce(ends[:], pre[:], AXIS_X, ALU.add))
                then_next(dve.tensor_tensor(behind[:], ends[0:1, None, :].to_broadcast(slots),
                                            tables[0:1, TAB_SLOT:TAB_SLOT + n_slots, None].to_broadcast(slots), ALU.is_le))
                dve.tensor_tensor(begun[:], behind[:], ends[0:1, None, :].to_broadcast(slots), ALU.mult)
                then_next(dve.tensor_reduce(slot_e[:], behind[:], AXIS_X, ALU.add))
                then_next(dve.tensor_reduce(slot_b[:], begun[:], AXIS_X, ALU.max))
                then_next(dve.tensor_tensor(slot_k[:], tables[0:1, TAB_SLOT:TAB_SLOT + n_slots], slot_b[:], ALU.subtract))
                dve.tensor_scalar(slot_k[:], slot_k[:], float(BLOCK), None, ALU.mult)
                then_next(dve.tensor_scalar(slot_r[:, 0, :], slot_e[:], float(n_experts - 1), None, ALU.min))
                then_next(dve.scalar_tensor_tensor(out=slot_r[:, 1, :], in0=slot_e[:], scalar=float(region), in1=slot_k[:],
                                                   op0=ALU.mult, op1=ALU.add))
                dve.tensor_copy(slot_i[:], slot_r[:]).then_inc(r_slot, 1)

                def prepare(s):
                    if s >= 2:
                        dve.wait_ge(f_t, s - 1)
                    for i in range(2):
                        row = r_ring[:, s % NR, i, :]
                        dve.wait_ge(f_z, 2 * s + i + 1)
                        ins = dve.tensor_scalar(xhat[:, s % 2, i, :], zz[:, s % 2, i, :], row[:, COL_S2:COL_S2 + 1],
                                                row[:, COL_T2:COL_T2 + 1], ALU.mult, ALU.add)
                    ins.then_inc(f_xh, 1)

                def split_xn(s):
                    dve.wait_ge(f_xa, s + 1)
                    if s >= 2:
                        dve.wait_ge(f_h, FC // 2 * (s - 1))
                    dve.tensor_copy(xn_hl[0][:, s % 2], xn[:]).then_inc(f_xd, 1)
                    dve.wait_ge(f_xd, 2 * s + 1)
                    dve.tensor_tensor(xn_hl[1][:, s % 2], xn[:], xn_hl[0][:, s % 2], ALU.subtract).then_inc(f_xd, 1)

                def low_weights(y, s):
                    dve.wait_ge(f_wh[y], s + 1)
                    if s >= NW:
                        weights_used(dve, y, s - NW)
                    part = slice(POOL_COLS, n_w)
                    dve.tensor_tensor(w_hl[y][1][:, s % NW, part], w_ring[y][:, s % NW, part], w_hl[y][0][:, s % NW, part],
                                      ALU.subtract).then_inc(f_wd[y], 1)

                def split_hid(s):
                    for half in range(2):
                        part = slice(half * FC // 2, (half + 1) * FC // 2)
                        dve.wait_ge(f_ha, FC * s + (half + 1) * FC // 2)
                        if s >= 2 and half == 0:
                            dve.wait_ge(f_y, 2 * s - 2)
                        dve.tensor_copy(hid_hl[0][:, s % 2, part, :], hid[:, part, :]).then_inc(f_hh, 1)
                        dve.wait_ge(f_hh, 2 * s + half + 1)
                        dve.tensor_tensor(hid_hl[1][:, s % 2, part, :], hid[:, part, :], hid_hl[0][:, s % 2, part, :], ALU.subtract).then_inc(f_hl, 1)

                def finish(s):
                    dve.wait_ge(f_y, 2 * s + 2)
                    dve.wait_ge(f_o, 2 * s)
                    for i in range(2):
                        dve.tensor_tensor(upd[:, i, :], upd_out(s)[:, i * d_model:(i + 1) * d_model], b2_ring[:, s % NR, :],
                                          ALU.add).then_inc(f_u, 1)
                    dve.wait_ge(f_base, s + 1)
                    if s >= 2:
                        dve.wait_ge(f_out[s % 2], 32 * (s // 2))
                    for i in range(2):
                        dve.wait_ge(f_u, 2 * s + i + 1)
                        dve.scalar_tensor_tensor(out=fin[:, s % 2, i, :], in0=upd[:, i, :],
                                                 scalar=r_ring[:, s % NR, i, COL_ALPHA:COL_ALPHA + 1],
                                                 in1=base[:, s % NR, i, :], op0=ALU.mult, op1=ALU.add).then_inc(f_o, 1)

                low_weights(0, 0)
                prepare(0)
                split_xn(0)
                prepare(1)
                low_weights(0, 1)
                split_hid(0)
                split_xn(1)
                low_weights(1, 0)
                for s in range(n_slots):
                    if s + 2 < n_slots:
                        low_weights(0, s + 2)
                        prepare(s + 2)
                    if s + 1 < n_slots:
                        split_hid(s + 1)
                    if s + 2 < n_slots:
                        split_xn(s + 2)
                    if s + 1 < n_slots:
                        low_weights(1, s + 1)
                    finish(s)


def kernel(x, ctx_1024, L0_xattn_ln_m_g, L0_xattn_ln_m_b, L0_xattn_ln_l_g, L0_xattn_ln_l_b, L0_xattn_Wq, L0_xattn_Wkv,
           L0_xattn_Wout, L0_ffn_centroids, L0_ffn_ln_g, L0_ffn_ln_b, L0_ffn_w1, L0_ffn_b1, L0_ffn_w2, L0_ffn_b2):
    import numpy as np
    import concourse.bacc as bacc
    from concourse.bass_utils import run_bass_kernel_spmd

    p = 128
    n_batches, n_tok, d_model = x.shape
    n_experts, d_ff, _ = L0_ffn_w1.shape
    kc, fc = d_model // p, d_ff // p
    n_tokens = n_batches * n_tok
    n_slots = n_tokens // BLOCK + n_experts - 1

    def columns(v):
        v = np.asarray(v)
        return np.swapaxes(v.reshape(*v.shape[:-1], -1, p), -1, -2)

    ln_pack = np.stack([columns(v) for v in (L0_xattn_ln_m_g, L0_xattn_ln_m_b, L0_xattn_ln_l_g, L0_xattn_ln_l_b)], axis=1)
    centroids_t = np.asarray(L0_ffn_centroids).T.reshape(kc, p, n_experts).transpose(1, 0, 2)
    w1 = np.asarray(L0_ffn_w1).transpose(0, 2, 1).reshape(n_experts, kc, p, d_ff).transpose(0, 2, 1, 3)
    w2 = np.asarray(L0_ffn_w2).transpose(0, 2, 1).reshape(n_experts, fc, p, d_model).transpose(0, 2, 1, 3)
    experts = np.concatenate([w1.reshape(n_experts, p, -1), w2.reshape(n_experts, p, -1),
                              columns(L0_ffn_ln_g), columns(L0_ffn_ln_b), columns(L0_ffn_b1)], axis=2)

    consts = np.zeros((p, 3 * p + N_TABLE + n_experts ** 2), np.float32)
    consts[:, 0:p] = np.eye(p)
    consts[:, p:2 * p] = np.triu(np.ones((p, p)), 1)
    consts[:, 2 * p:3 * p] = 1.0
    tables = consts[:, 3 * p:3 * p + N_TABLE]
    tables[:, TAB_RANK:TAB_RANK + n_experts] = n_experts - np.arange(n_experts)
    tables[:, TAB_REGION:TAB_REGION + n_experts] = (n_tokens + BLOCK) * np.arange(n_experts)
    tables[:, TAB_BLOCK:TAB_BLOCK + n_tokens // BLOCK] = BLOCK * np.arange(n_tokens // BLOCK)
    tables[:, TAB_SLOT:TAB_SLOT + n_slots] = np.arange(n_slots)
    tables[:, TAB_TOKEN:TAB_TOKEN + n_batches] = np.arange(n_batches)[None, :] * p + np.arange(p)[:, None]
    consts[:, 3 * p + N_TABLE:] = np.tril(np.ones((n_experts, n_experts))).reshape(-1)

    arrays = {"x": x, "ctx_in": ctx_1024, "ln_pack": ln_pack, "w_q": L0_xattn_Wq, "w_kv": L0_xattn_Wkv,
              "w_out": L0_xattn_Wout, "centroids_t": centroids_t, "consts": consts, "experts": experts, "b2": L0_ffn_b2}
    arrays = {f"in_{k}": np.ascontiguousarray(v) for k, v in arrays.items()}
    nc = bacc.Bacc("TRN2", target_bir_lowering=False, num_devices=1)
    args = [nc.dram_tensor(k, v.shape, mybir.dt.from_np(v.dtype), kind="ExternalInput").ap() for k, v in arrays.items()]
    out = nc.dram_tensor("out", (n_batches * n_tok, d_model), F32, kind="ExternalOutput").ap()
    build(nc, *args, out)
    r = run_bass_kernel_spmd(nc, [arrays], core_ids=[0])
    return r.results[0]["out"].reshape(n_batches, n_tok, d_model)
```

```python
import math
from contextlib import ExitStack, nullcontext

import concourse.bass as bass
from concourse import mybir

F32 = mybir.dt.float32
F32R = mybir.dt.float32r
I32 = mybir.dt.int32
ACT = mybir.ActivationFunctionType
ALU = mybir.AluOpType
AXIS_X = mybir.AxisListType.X

P = 128
DH = 64
EPS = 1e-5
BANK = 512
OUT_OF_RANGE = 1 << 20

BLOCK = 2 * P
FILL = BLOCK + 2 * P

COL_S1, COL_T1, COL_S2, COL_T2, COL_ALPHA, COL_TOKEN = range(256, 262)
ROW = 264

TAB_RANK, TAB_REGION, TAB_BLOCK, TAB_SLOT, TAB_TOKEN, N_TABLE = 0, 16, 32, 64, 96, 128

PASSES = ((0, 0), (0, 1), (1, 0))


def plan_jobs(n_batches):
    before = [("ln", 0, 0), ("ln", 1, 0)]
    before += [(kind, 0, m) for m in range(4) for kind in "kv"] + [("q", 0, m) for m in range(4)]
    beside = []
    for b in range(n_batches):
        work = []
        if b + 1 < n_batches:
            work += [("k", b + 1, m) for m in range(4)] + [("v", b + 1, m) for m in range(4)]
        for s in range(4):
            if b % 2 == 1:
                part = work[(0, 3, 4, 6)[s]:(3, 4, 6, 8)[s]]
                if b + 1 < n_batches and s >= 1:
                    part = [("q", (b + 1) // 2, s - 1)] + part
            else:
                part = work[2 * s:2 * s + 2]
                if b >= 2 and s == 0:
                    part = [("q", b // 2, 3)] + part
                if b + 2 < n_batches and s >= 2:
                    part = part[:1] + [("ln", b + s, 0)] + part[1:]
            kind, of = (("aff", b - 2), ("rank", b - 2), ("wout", b - 1), ("zt", b - 1))[s]
            if of >= 0:
                at = (0, 0, 1, 1)[s]
                part = part[:at] + [(kind, of, 0)] + part[at:]
            if of == n_batches - 3 and kind == "rank":
                part = part + [("tails", of, 0)]
            beside.append((part[:1], part[1:2], part[2:]))
    beside += [([("aff", n_batches - 2, 0)], [], []), ([("rank", n_batches - 2, 0)], [], [])]
    after = [("wout", n_batches - 1, 0), ("zt", n_batches - 1, 0), ("aff", n_batches - 1, 0), ("rank", n_batches - 1, 0)]
    return before, beside, after


def build(nc, x, ctx_in, ln_pack, w_q, w_kv, w_out, centroids_t, consts, experts, b2, out):
    n_batches, _, d_model = x.shape
    inner = w_q.shape[1]
    n_experts = centroids_t.shape[2]
    KC = d_model // P
    d_ff = (experts.shape[2] - 2 * KC) * P // (2 * KC * P + 1)
    HC = inner // P
    FC = d_ff // P
    n_tiles = n_batches
    n_tokens = n_tiles * P
    n_slots = n_tokens // BLOCK + n_experts - 1
    region = n_tokens + BLOCK
    n_quads = n_batches * 4
    before, beside, after = plan_jobs(n_batches)
    all_jobs = before + [j for parts in beside for j in sum(parts, [])] + after
    number = {job: i for i, job in enumerate(all_jobs)}
    half_number = {}
    for job in all_jobs:
        if job[0] in "qk":
            half_number[job] = max(half_number.values(), default=0) + (1 if job[0] == "q" else 2)

    sorted_rows = nc.dram_tensor("sorted_rows", [n_experts * region, ROW], F32, kind="Internal").ap()

    with ExitStack() as top:
        def sem(name):
            return top.enter_context(nc.semaphore(name))

        def sbuf(scope, name, shape, dtype=F32):
            return scope.enter_context(nc.sbuf_tensor(name, shape, dtype))

        psum = top.enter_context(nc.psum_tensor("psum", [P, 8, BANK], F32))
        ident = sbuf(top, "ident", [P, P])
        lower_ones = sbuf(top, "lower_ones", [P, 2, P])
        tables = sbuf(top, "tables", [P, N_TABLE])
        prefix = sbuf(top, "prefix", [P, n_experts, n_experts])
        onehot = sbuf(top, "onehot", [P, 2, n_experts])
        counts = sbuf(top, "counts", [P, 2, n_experts])
        best = sbuf(top, "best", [P, 2])
        filler = sbuf(top, "filler", [P, ROW])

        slot_i = sbuf(top, "slot_i", [1, 2, n_slots], I32)
        empty_i = sbuf(top, "empty_i", [1, 1], I32)

        with ExitStack() as a:
            w_split = [sbuf(a, f"w_{h}", [P, KC, 3 * inner], F32R) for h in ("hi", "lo")]
            kv_t = [sbuf(a, f"kv_t_{h}", [P, KC, 4, 2 * P], F32R) for h in ("hi", "lo")]
            w_o = [sbuf(a, f"w_o_{h}", [P, HC, d_model], F32R) for h in ("hi", "lo")]
            q_t = [sbuf(a, f"q_t_{h}", [P, HC, 2 * P], F32R) for h in ("hi", "lo")]
            q_twice = sbuf(a, "q_twice", [P, 2 * HC, 2 * P], F32R)
            k_both = sbuf(a, "k_both", [P, 2, 2 * HC, 2 * P], F32R)
            v_n = sbuf(a, "v_n", [P, 2, 2, inner])
            y_t = sbuf(a, "y_t", [P, KC, 2, P])
            NPROB = 4
            prob = sbuf(a, "prob", [P, NPROB, 2, 2 * P])
            NPT = 4
            prob_t = sbuf(a, "prob_t", [P, NPT, 2, 2, P])
            head_out = [sbuf(a, f"head_out_{h}", [P, HC, P], F32R) for h in ("hi", "lo")]
            NROW = 3
            row_ring = sbuf(a, "row_ring", [P, NROW, ROW])
            place = sbuf(a, "place", [P, 2, n_experts])
            place_f = sbuf(a, "place_f", [P, 1])
            place_i = sbuf(a, "place_i", [P, NROW], I32)
            gate = sbuf(a, "gate", [P, 2, 2])
            NX, NCTX = 6, 2
            x_in = sbuf(a, "x_in", [P, NX, d_model])
            c_in = sbuf(a, "c_in", [P, NCTX, d_model])
            normed = sbuf(a, "normed", [P, 4, d_model])
            z_buf = sbuf(a, "z_buf", [P, d_model])
            z_t = sbuf(a, "z_t", [P, KC, P])
            cent = sbuf(a, "cent", [P, KC, n_experts])
            ln_w = sbuf(a, "ln_w", [P, 4, KC])
            stats = sbuf(a, "stats", [P, 4, 6])
            mean_var = sbuf(a, "mean_var", [P, 4, 2])
            ln_scale = sbuf(a, "ln_scale", [P, 2, 4])
            ln_shift = sbuf(a, "ln_shift", [P, 2, 4])
            tmp_v = sbuf(a, "tmp_v", [P, 4])
            var_eps = sbuf(a, "var_eps", [P, 4])
            minus_half = sbuf(a, "minus_half", [P, 4])
            neg_max = sbuf(a, "neg_max", [P, 8, 2])
            prob_sum = sbuf(a, "prob_sum", [P, 8, 2])
            inv_sum = sbuf(a, "inv_sum", [P, 8, 2])
            stats_z = sbuf(a, "stats_z", [P, 2, 6])
            mv_z = sbuf(a, "mv_z", [P, 2, 2])
            aff = sbuf(a, "aff", [P, 2, n_experts])
            rank_w = sbuf(a, "rank_w", [P, n_experts])
            rank_m = sbuf(a, "rank_m", [P, 1])
            tail_f = sbuf(a, "tail_f", [1, n_experts])
            tail_i = sbuf(a, "tail_i", [1, n_experts], I32)

            s_early = sem("s_early")
            s_const = sem("s_const")
            s_in = [sem("s_in0"), sem("s_in1")]
            s_w = [sem(f"s_w{i}") for i in range(3)]
            s_wo = sem("s_wo")
            s_whi = sem("s_whi")
            s_wlo = sem("s_wlo")
            s_wo_split = sem("s_wo_split")
            s_lnp = sem("s_lnp")
            s_mv = sem("s_mv")
            s_mv1 = sem("s_mv1")
            s_mv2 = sem("s_mv2")
            s_st1 = sem("s_st1")
            s_st2 = sem("s_st2")
            s_pool = sem("s_pool")
            s_nrm = sem("s_nrm")
            s_job = sem("s_job")
            s_bank = [sem("s_bank0"), sem("s_bank1")]
            s_hi = sem("s_hi")
            s_lo = sem("s_lo")
            s_score = sem("s_score")
            s_max = sem("s_max")
            s_exp = sem("s_exp")
            s_inv = sem("s_inv")
            s_soft = sem("s_soft")
            s_tr = sem("s_tr")
            s_pt = sem("s_pt")
            s_pv = sem("s_pv")
            s_hoh = sem("s_hoh")
            s_ho = sem("s_ho")
            s_twice = [sem(f"s_twice{m}") for m in range(4)]
            s_half = sem("s_half")
            s_oh = sem("s_oh")
            s_gate = sem("s_gate")
            s_pos = sem("s_pos")
            s_scat = [sem(f"s_scat{i}") for i in range(NROW)]
            s_z = sem("s_z")
            s_dve = sem("s_dve")
            s_pad = sem("s_pad")
            s_total = sem("s_total")
            s_tail = sem("s_tail")
            w_raw = [v_n[:, 0].rearrange("p s n -> p (s n)"), v_n[:, 1].rearrange("p s n -> p (s n)"),
                     prob[:].rearrange("p n i j -> p (n i j)")[:, 0:KC * inner]]
            w_raw = [w.rearrange("p (c n) -> p c n", c=KC) for w in w_raw]
            w_cols = [slice(i * inner, (i + 1) * inner) for i in (1, 2, 0)]
            w_o_raw = prob_t[:].rearrange("p n i s t -> p (n i s t)")[:, 0:HC * d_model]

            n_over = n_tokens // BLOCK
            scratch_at = [0]

            def scratch(*dims):
                size = math.prod(dims)
                flat = normed[:].rearrange("p j d -> p (j d)")[:, scratch_at[0]:scratch_at[0] + size]
                scratch_at[0] += size
                return flat if len(dims) == 1 else flat.rearrange("p (a b) -> p a b", a=dims[0])

            over = scratch(n_experts, n_over)
            blocks_e = scratch(n_experts)
            pre = scratch(n_experts, n_experts)
            ends = scratch(n_experts)
            total_e = scratch(n_experts)
            behind = scratch(n_slots, n_experts)[0:1]
            begun = scratch(n_slots, n_experts)[0:1]
            empty_f = scratch(1)[0:1]
            slot_e, slot_b, slot_k, slot_r = (scratch(n_slots)[0:1] for _ in range(4))

            block = a.enter_context(nc.Block())

            def unit_bank(n):
                return n % 3

            def tr_bank(n):
                return 3 + n % 2

            OUT_BANK = 5

            def job_bank(j):
                return psum[:, 6 + j % 2, :]

            def wait_read(eng, job):
                j = number[job]
                eng.wait_ge(s_bank[j % 2], j // 2 + 1)

            def wait_job(eng, job):
                eng.wait_ge(s_job, number[job] + 1)

            def unit_heads(n):
                quad, parity = n // 2, n % 2
                h0 = 4 * (quad % 4) + parity
                return quad // 4, (h0, h0 + 2)

            @block.sync
            def _(sp):
                def load_pair(g):
                    if g >= 1:
                        sp.wait_ge(s_nrm, g)
                    if g >= 3:
                        sp.wait_ge(s_z, 2 * (g - 3) + 2)
                    b = 2 * g
                    sp.dma_start(x_in[:, b % NX:b % NX + 2, :],
                                 x[b:b + 2].rearrange("b p d -> p b d")).then_inc(s_in[g % 2], 16)
                    sp.dma_start(c_in[:, b % NCTX:b % NCTX + 2, :],
                                 ctx_in[b:b + 2].rearrange("b p d -> p b d")).then_inc(s_in[g % 2], 16)

                load_pair(0)
                sp.dma_start(ident[:], consts[:, 0:P]).then_inc(s_early, 16)
                sp.dma_start(ln_w[:], ln_pack).then_inc(s_early, 16)
                for i, src in enumerate((w_kv[:, 0:inner], w_kv[:, inner:2 * inner], w_q)):
                    sp.dma_start(w_raw[i],
                                 src.rearrange("(c p) n -> p c n", p=P)).then_inc(s_w[i], 16)
                sp.dma_start(w_o_raw.rearrange("p (c n) -> p c n", c=HC), w_out.rearrange("(c p) n -> p c n", p=P)).then_inc(s_wo, 16)
                sp.dma_start(lower_ones[:], consts[:, P:3 * P].rearrange("p (a b) -> p a b", a=2)).then_inc(s_const, 16)
                sp.dma_start(tables[:], consts[:, 3 * P:3 * P + N_TABLE]).then_inc(s_const, 16)
                sp.dma_start(prefix[:], consts[:, 3 * P + N_TABLE:].rearrange("p (a b) -> p a b", a=n_experts)).then_inc(s_const, 16)
                sp.dma_start(cent[:], centroids_t).then_inc(s_const, 16)
                def repeat_queries(g):
                    for m in range(4):
                        sp.wait_ge(s_half, half_number[("q", g, m)])
                        if g >= 1:
                            sp.wait_ge(s_score, 2 * (8 * g - 4 + m) + 2)
                        for parity in range(2):
                            for dst_lo in (0, DH):
                                sp.dma_start(q_twice.bitcast(F32)[dst_lo:dst_lo + DH, 4 * m + parity:4 * m + 4:2, :],
                                             q_t[0].bitcast(F32)[parity * DH:(parity + 1) * DH, 2 * m:2 * m + 2, :]
                                             ).then_inc(s_twice[m], 16)

                for g in range(n_batches // 2):
                    if g + 1 < n_batches // 2:
                        load_pair(g + 1)
                    repeat_queries(g)
                for m in range(4):
                    sp.wait_ge(s_twice[m], 64 * (n_batches // 2))
                sp.wait_ge(s_pad, 2)
                wait_read(sp, ("tails", n_batches - 3, 0))
                for e in range(n_experts):
                    first = sp.value_load(tail_i[0:1, e:e + 1], min_val=0, max_val=n_experts * region - FILL)
                    sp.dma_start(sorted_rows[bass.DynSlice(first, FILL), :].rearrange("(a p) c -> p a c", p=P),
                                 filler[:, None, :].to_broadcast([P, FILL // P, ROW])).then_inc(s_tail, 16)
                sp.wait_ge(s_tail, 16 * n_experts)

            @block.tensor
            def _(pe):
                def run_job(job):
                    kind, b, m = job
                    j = number[job]
                    bank = job_bank(j)
                    if j >= 2:
                        pe.wait_ge(s_bank[j % 2], j // 2)
                    if kind == "ln":
                        pe.wait_ge(s_nrm, b // 2 + 1)
                        for c in range(KC):
                            for side in range(2):
                                last = pe.transpose(bank[:, (2 * c + side) * P:(2 * c + side + 1) * P],
                                                    normed[:, 2 * side + b % 2, c * P:(c + 1) * P], ident[:])
                    elif kind in "qk":
                        first_b = 2 * b if kind == "q" else b
                        pe.wait_ge(s_hi, (2 * b + 2) if kind == "q" else b + 1)
                        pe.wait_ge(s_lo, (2 * b + 2) if kind == "q" else b + 1)
                        slot = first_b % 4
                        for cc in range(2):
                            col = (inner if kind == "k" else 0) + (2 * m + cc) * P
                            for i, (hw, hx) in enumerate(PASSES):
                                for c in range(KC):
                                    tokens = (kv_t[hx][:, c, slot, :] if kind == "k" else
                                              kv_t[hx][:, c, slot:slot + 2, P:2 * P])
                                    dst = bank[:, cc * 2 * P:(cc + 1) * 2 * P]
                                    if kind == "q":
                                        dst = dst.rearrange("p (a t) -> p a t", a=2)
                                    last = pe.matmul(dst, w_split[hw][:, c, col:col + P], tokens,
                                                     start=(i == 0 and c == 0), stop=(i == 2 and c == KC - 1))
                    elif kind == "v":
                        side, half = m // 2, m % 2
                        slot = b % 4
                        for i, (hx, hw) in enumerate(PASSES):
                            for c in range(KC):
                                last = pe.matmul(bank, kv_t[hx][:, c, slot, side * P:(side + 1) * P],
                                                 w_split[hw][:, c, 2 * inner + half * BANK:2 * inner + (half + 1) * BANK],
                                                 start=(i == 0 and c == 0), stop=(i == 2 and c == KC - 1))
                    elif kind == "wout":
                        pe.wait_ge(s_ho, 2 * b + 2)
                        for i, (ho, hw) in enumerate(PASSES):
                            for c in range(HC):
                                last = pe.matmul(bank[:, 0:d_model], head_out[ho][:, c, :], w_o[hw][:, c, :],
                                                 start=(i == 0 and c == 0), stop=(i == 2 and c == HC - 1))
                    elif kind == "zt":
                        pe.wait_ge(s_z, b + 1)
                        for c in range(KC):
                            last = pe.transpose(bank[:, c * P:(c + 1) * P], z_buf[:, c * P:(c + 1) * P], ident[:])
                    elif kind == "tails":
                        last = pe.matmul(bank[:, 0:n_experts], lower_ones[:, 1, :], counts[:, (b + 1) % 2, :],
                                         start=True, stop=True)
                    elif kind == "rank":
                        pe.wait_ge(s_oh, b + 1)
                        pe.matmul(bank[:, 0:n_experts], lower_ones[:, 0, :], onehot[:, b % 2, :], start=True, stop=False)
                        last = pe.matmul(bank[:, 0:n_experts], lower_ones[:, 1, :], counts[:, b % 2, :], start=False, stop=True)
                    else:
                        wait_read(pe, ("zt", b, 0))
                        for c in range(KC):
                            last = pe.matmul(bank[:, 0:n_experts], z_t[:, c, :], cent[:, c, :],
                                             start=(c == 0), stop=(c == KC - 1))
                    last.then_inc(s_job, 1)

                def scores(quad):
                    b = quad // 4
                    m = quad % 4
                    wait_read(pe, ("k", b, m))
                    if b % 2 == 0:
                        wait_read(pe, ("q", b // 2, m))
                        pe.wait_ge(s_twice[m], 64 * (b // 2 + 1))
                    for n in (2 * quad, 2 * quad + 1):
                        if n >= 3:
                            pe.wait_ge(s_exp, 2 * (n - 3) + 2)
                    tokens = slice((b % 2) * P, (b % 2 + 1) * P)
                    for i in range(2):
                        for n in (2 * quad, 2 * quad + 1):
                            h = unit_heads(n)[1][i]
                            pe.matmul(psum[:, unit_bank(n), i * 2 * P:(i + 1) * 2 * P],
                                      q_twice[:, h, tokens], k_both[:, b % 2, h, :], start=True, stop=False)
                        for n in (2 * quad, 2 * quad + 1):
                            h = unit_heads(n)[1][i]
                            lo = DH * (h % 2)
                            ins = pe.matmul(psum[:, unit_bank(n), i * 2 * P:(i + 1) * 2 * P],
                                            q_t[1][lo:lo + DH, h // 2, tokens],
                                            k_both[lo:lo + DH, b % 2, h, :], start=False, stop=True)
                            if i == 1:
                                ins.then_inc(s_score, 1)

                def transposes(n):
                    pe.wait_ge(s_soft, n + 1)
                    if n >= 2:
                        pe.wait_ge(s_pt, n - 1)
                    for i in range(2):
                        for side in range(2):
                            last = pe.transpose(psum[:, tr_bank(n), (2 * i + side) * P:(2 * i + side + 1) * P],
                                                prob[:, n % NPROB, i, side * P:(side + 1) * P], ident[:])
                    last.then_inc(s_tr, 1)

                def outputs(quad):
                    b = quad // 4
                    if quad % 2 == 0:
                        for side in range(2):
                            wait_read(pe, ("v", b, 2 * side + quad % 4 // 2))
                    pe.wait_ge(s_pt, 2 * quad + 2)
                    if quad % 2 == 0 and quad >= 2:
                        pe.wait_ge(s_ho, quad // 2)
                    for i in range(2):
                        for side in range(2):
                            for n in (2 * quad, 2 * quad + 1):
                                h = unit_heads(n)[1][i]
                                lo = DH * (h % 2)
                                slot = (h // 2) % 4
                                last = pe.matmul(psum[lo:lo + DH, OUT_BANK, slot * P:(slot + 1) * P],
                                                 v_n[:, b % 2, side, h * DH:(h + 1) * DH],
                                                 prob_t[:, n % NPT, i, side, :],
                                                 start=(side == 0), stop=(side == 1))
                    last.then_inc(s_pv, 1)

                pe.wait_ge(s_early, 2 * 16)
                for job in before:
                    if job[0] in "kvq":
                        pe.wait_ge(s_whi, "kvq".index(job[0]) + 1)
                        pe.wait_ge(s_wlo, "kvq".index(job[0]) + 1)
                    run_job(job)
                pe.wait_ge(s_const, 4 * 16)
                pe.wait_ge(s_wo_split, 2)
                for t in range(n_quads + 2):
                    first, second, rest = beside[t]
                    if t < n_quads:
                        scores(t)
                    for job in first:
                        run_job(job)
                    if t >= 2:
                        outputs(t - 2)
                    for job in second:
                        run_job(job)
                    if 1 <= t <= n_quads:
                        transposes(2 * t - 2)
                        transposes(2 * t - 1)
                    for job in rest:
                        run_job(job)
                for job in after:
                    run_job(job)
                j = len(all_jobs)
                pe.wait_ge(s_bank[j % 2], j // 2)
                pe.matmul(job_bank(j)[:, 0:n_experts], lower_ones[:, 1, :], counts[:, n_tiles % 2, :],
                          start=True, stop=True).then_inc(s_total, 1)

            @block.scalar
            def _(act):
                def normalise(g):
                    act.wait_ge(s_lnp, g + 1)
                    if g >= 1:
                        wait_job(act, ("ln", 2 * g - 1, 0))
                    for j in range(4):
                        side, b = j // 2, 2 * g + j % 2
                        src = c_in[:, b % NCTX, :] if side == 0 else x_in[:, b % NX, :]
                        last = act.activation(normed[:, j, :], src, ACT.Identity,
                                              bias=ln_shift[:, g % 2, j:j + 1], scale=ln_scale[:, g % 2, j:j + 1])
                    last.then_inc(s_nrm, 1)

                def read_job(job):
                    kind, b, m = job
                    if kind not in ("ln", "q", "k", "v"):
                        return
                    j = number[job]
                    bank = job_bank(j)
                    wait_job(act, job)
                    if kind == "ln":
                        if b >= 1:
                            act.wait_ge(s_lo, b)
                        for c in range(KC):
                            for side in range(2):
                                last = act.activation(y_t[:, c, side, :],
                                                      bank[:, (2 * c + side) * P:(2 * c + side + 1) * P], ACT.Identity,
                                                      bias=ln_w[:, 2 * side + 1, c:c + 1], scale=ln_w[:, 2 * side, c:c + 1])
                    elif kind == "q":
                        if b >= 1:
                            act.wait_ge(s_twice[m], 64 * b)
                        last = act.activation(q_t[0][:, 2 * m:2 * m + 2, :].rearrange("p c t -> p (c t)"), bank,
                                              ACT.Copy, scale=DH ** -0.5)
                    elif kind == "k":
                        if b >= 2:
                            act.wait_ge(s_score, 8 * (b - 1))
                        for parity in range(2):
                            rows = slice(parity * DH, (parity + 1) * DH)
                            last = act.activation(k_both[rows, b % 2, 4 * m + parity:4 * m + 4:2, :],
                                                  bank[rows, :].rearrange("p (c t) -> p c t", c=2), ACT.Copy)
                            if parity == 0:
                                last.then_inc(s_half, 1)
                    else:
                        if b >= 2:
                            act.wait_ge(s_pv, 4 * (b - 1))
                        last = act.activation(v_n[:, b % 2, m // 2, (m % 2) * BANK:(m % 2 + 1) * BANK], bank, ACT.Copy)
                    last.then_inc(s_half if kind in "qk" else s_bank[j % 2], 1)

                def exponentials(n):
                    act.wait_ge(s_max, n + 1)
                    if n >= NPROB:
                        act.wait_ge(s_tr, n - NPROB + 1)
                    for i in range(2):
                        act.activation(prob[:, n % NPROB, i, :], psum[:, unit_bank(n), i * 2 * P:(i + 1) * 2 * P], ACT.Exp,
                                       bias=neg_max[:, n % 8, i:i + 1],
                                       accum_out=prob_sum[:, n % 8, i:i + 1]).then_inc(s_exp, 1)

                def copy_outputs(half):
                    act.wait_ge(s_pv, 2 * half + 2)
                    b = half // 2
                    if b >= 1 and half % 2 == 0:
                        wait_job(act, ("wout", b - 1, 0))
                    act.activation(head_out[0][:, 4 * (half % 2):4 * (half % 2) + 4, :].rearrange("p c t -> p (c t)"),
                                   psum[:, OUT_BANK, :], ACT.Copy).then_inc(s_hoh, 1)

                def norm_x1(b):
                    act.wait_ge(s_st1, b + 1)
                    if b >= 1:
                        wait_job(act, ("zt", b - 1, 0))
                        act.wait_ge(s_mv2, b)
                    row = row_ring[:, b % NROW, :]
                    act.activation(z_buf[:], row[:, 0:d_model], ACT.Identity, bias=row[:, COL_T1:COL_T1 + 1],
                                   scale=row[:, COL_S1:COL_S1 + 1]).then_inc(s_z, 1)

                def gate_of(b):
                    act.wait_ge(s_oh, b + 1)
                    if b >= 2:
                        act.wait_ge(s_pos, b - 1)
                    act.activation(gate[:, 0, b % 2:b % 2 + 1], best[:, b % 2:b % 2 + 1], ACT.Exp, scale=-1.0).then_inc(s_gate, 1)

                def high_weights(i):
                    act.wait_ge(s_w[i], 16)
                    act.activation(w_split[0][:, :, w_cols[i]], w_raw[i], ACT.Copy).then_inc(s_whi, 1)

                high_weights(0)
                act.wait_ge(s_early, 2 * 16)
                normalise(0)
                high_weights(1)
                read_job(before[0])
                high_weights(2)
                read_job(before[1])
                for job in before[2:]:
                    read_job(job)
                for t in range(n_quads + 2):
                    first, second, rest = beside[t]
                    for kind, b, _ in first + second + rest:
                        if kind == "rank":
                            gate_of(b)
                    if t < n_quads:
                        exponentials(2 * t)
                    for job in first:
                        read_job(job)
                    if t < n_quads:
                        exponentials(2 * t + 1)
                    for job in second:
                        read_job(job)
                    if t >= 3 and t % 2 == 1:
                        copy_outputs((t - 3) // 2)
                    for job in rest:
                        read_job(job)
                    for kind, b, _ in first + second + rest:
                        if kind == "wout":
                            norm_x1(b)
                    b = t // 4
                    if t % 8 == 1 and b + 2 < n_batches:
                        normalise(b // 2 + 1)
                norm_x1(n_batches - 1)
                gate_of(n_batches - 1)

            @block.vector
            def _(dve):
                chained = [0]

                def then_next(ins):
                    chained[0] += 1
                    ins.then_inc(s_dve, 1)
                    dve.wait_ge(s_dve, chained[0])

                def layer_norm_stats(g, j):
                    if j == 0:
                        dve.wait_ge(s_in[g % 2], 32 * (g // 2 + 1))
                        if g >= 1:
                            dve.wait_ge(s_lnp, g)
                    side, b = j // 2, 2 * g + j % 2
                    src = c_in[:, b % NCTX, :] if side == 0 else x_in[:, b % NX, :]
                    then_next(dve.bn_stats(stats[:, j, :], src))
                    dve.bn_aggr(mean_var[:, j, :], stats[:, j, :]).then_inc(s_mv, 1)

                def maxima(n):
                    dve.wait_ge(s_score, n + 1)
                    dve.tensor_reduce(neg_max[:, n % 8, :], psum[:, unit_bank(n), :].rearrange("p (i j) -> p i j", i=2),
                                      AXIS_X, ALU.max, negate=True).then_inc(s_max, 1)

                def inverse_sums(n):
                    dve.wait_ge(s_exp, 2 * n + 2)
                    dve.reciprocal(inv_sum[:, n % 8, :], prob_sum[:, n % 8, :]).then_inc(s_inv, 1)

                def copy_transposed(n):
                    dve.wait_ge(s_tr, n + 1)
                    if n >= NPT:
                        dve.wait_ge(s_pv, (n - NPT) // 2 + 1)
                    dve.tensor_copy(prob_t[:, n % NPT].rearrange("p i s t -> p (i s t)"), psum[:, tr_bank(n), :]).then_inc(s_pt, 1)

                def read_job(job):
                    kind, b, m = job
                    j = number[job]
                    bank = job_bank(j)
                    if kind == "ln":
                        wait_read(dve, job)
                        if b >= 4:
                            wait_job(dve, ("v", b - 4, 3))
                            wait_job(dve, ("q", (b - 4) // 2, 3))
                        dve.tensor_copy(kv_t[0][:, :, b % 4, :].rearrange("p c (s t) -> p c s t", s=2), y_t[:]).then_inc(s_hi, 1)
                    elif kind in "qk":
                        if kind == "q":
                            dve.wait_ge(s_half, half_number[job])
                            if b >= 1:
                                dve.wait_ge(s_score, 2 * (8 * b - 4 + m) + 2)
                            hi, lo = [q[:, 2 * m:2 * m + 2, :].rearrange("p c t -> p (c t)") for q in q_t]
                            ins = dve.scalar_tensor_tensor(out=lo, in0=bank, scalar=DH ** -0.5, in1=hi,
                                                           op0=ALU.mult, op1=ALU.subtract)
                        else:
                            for parity in range(2):
                                dve.wait_ge(s_half, half_number[job] - 1 + parity)
                                heads = k_both[:, b % 2, 4 * m + parity:4 * m + 4:2, :]
                                hi, lo = slice(parity * DH, (parity + 1) * DH), slice((1 - parity) * DH, (2 - parity) * DH)
                                ins = dve.tensor_tensor(heads[lo], bank[hi, :].rearrange("p (c t) -> p c t", c=2), heads[hi],
                                                        ALU.subtract)
                        ins.then_inc(s_bank[j % 2], 1)
                    elif kind == "wout":
                        wait_job(dve, job)
                        if b >= NROW:
                            dve.wait_ge(s_scat[b % NROW], 16 * (b // NROW))
                        x1 = row_ring[:, b % NROW, 0:d_model]
                        ins = dve.tensor_tensor(x1, bank[:, 0:d_model], x_in[:, b % NX, :], ALU.add)
                        ins.then_inc(s_bank[j % 2], 1)
                        dve.wait_ge(s_bank[j % 2], j // 2 + 1)
                        then_next(dve.bn_stats(stats_z[:, 0, :], x1))
                        if b >= 1:
                            dve.wait_ge(s_st1, b)
                        dve.bn_aggr(mv_z[:, 0, :], stats_z[:, 0, :]).then_inc(s_mv1, 1)
                    elif kind == "zt":
                        wait_job(dve, job)
                        if b >= 1:
                            wait_job(dve, ("aff", b - 1, 0))
                        dve.tensor_copy(z_t[:].rearrange("p c t -> p (c t)"), bank[:, 0:KC * P]).then_inc(s_bank[j % 2], 1)
                        dve.wait_ge(s_z, b + 1)
                        then_next(dve.bn_stats(stats_z[:, 1, :], z_buf[:]))
                        if b >= 1:
                            dve.wait_ge(s_st2, b)
                        dve.bn_aggr(mv_z[:, 1, :], stats_z[:, 1, :]).then_inc(s_mv2, 1)
                    elif kind == "aff":
                        wait_job(dve, job)
                        if b >= 1:
                            wait_job(dve, ("rank", b - 1, 0))
                            dve.wait_ge(s_pos, b)
                        scores_b, same = aff[:, 0, :], aff[:, 1, :]
                        dve.tensor_copy(scores_b, bank[:, 0:n_experts]).then_inc(s_bank[j % 2], 1)
                        dve.wait_ge(s_bank[j % 2], j // 2 + 1)
                        then_next(dve.tensor_reduce(best[:, b % 2:b % 2 + 1], scores_b, AXIS_X, ALU.max))
                        then_next(dve.tensor_scalar(same, scores_b, best[:, b % 2:b % 2 + 1], None, ALU.is_equal))
                        then_next(dve.tensor_tensor(rank_w[:], same, tables[:, TAB_RANK:TAB_RANK + n_experts], ALU.mult))
                        then_next(dve.tensor_reduce(rank_m[:], rank_w[:], AXIS_X, ALU.max))
                        then_next(dve.tensor_scalar(onehot[:, b % 2, :], rank_w[:], rank_m[:, 0:1], None, ALU.is_equal))
                        dve.tensor_tensor(counts[:, (b + 1) % 2, :], counts[:, b % 2, :], onehot[:, b % 2, :], ALU.add).then_inc(s_oh, 1)
                        dve.wait_ge(s_oh, b + 1)
                    elif kind == "tails":
                        wait_job(dve, job)
                        then_next(dve.tensor_tensor(tail_f[:], bank[0:1, 0:n_experts],
                                                    tables[0:1, TAB_REGION:TAB_REGION + n_experts], ALU.add))
                        dve.tensor_copy(tail_i[:], tail_f[:]).then_inc(s_bank[j % 2], 1)
                    elif kind == "rank":
                        wait_job(dve, job)
                        row = row_ring[:, b % NROW, :]
                        dve.tensor_tensor(place[:, 0, :], bank[:, 0:n_experts], tables[:, TAB_REGION:TAB_REGION + n_experts],
                                          ALU.add).then_inc(s_bank[j % 2], 1)
                        dve.wait_ge(s_bank[j % 2], j // 2 + 1)
                        dve.tensor_copy(row.bitcast(I32)[:, COL_TOKEN:COL_TOKEN + 1], tables[:, TAB_TOKEN + b:TAB_TOKEN + b + 1])
                        then_next(dve.tensor_tensor(place[:, 1, :], place[:, 0, :], onehot[:, b % 2, :], ALU.mult))
                        dve.wait_ge(s_gate, b + 1)
                        dve.tensor_scalar(gate[:, 1, b % 2:b % 2 + 1], gate[:, 0, b % 2:b % 2 + 1], 1.0, None, ALU.add)
                        then_next(dve.tensor_reduce(place_f[:], place[:, 1, :], AXIS_X, ALU.add))
                        dve.reciprocal(row[:, COL_ALPHA:COL_ALPHA + 1], gate[:, 1, b % 2:b % 2 + 1])
                        dve.tensor_copy(place_i[:, b % NROW:b % NROW + 1], place_f[:]).then_inc(s_pos, 1)

                def low_outputs(half):
                    dve.wait_ge(s_hoh, half + 1)
                    part = slice(4 * (half % 2), 4 * (half % 2) + 4)
                    dve.tensor_tensor(head_out[1][:, part, :].rearrange("p c t -> p (c t)"), psum[:, OUT_BANK, :],
                                      head_out[0][:, part, :].rearrange("p c t -> p (c t)"), ALU.subtract).then_inc(s_ho, 1)

                dve.memset(row_ring[:, :, COL_TOKEN + 1:], 0.0)
                then_next(dve.memset(counts[:, 0, :], 0.0))
                for j in range(4):
                    layer_norm_stats(0, j)
                def low_weights(i):
                    dve.wait_ge(s_whi, i + 1)
                    dve.tensor_tensor(w_split[1][:, :, w_cols[i]], w_raw[i], w_split[0][:, :, w_cols[i]],
                                      ALU.subtract).then_inc(s_wlo, 1)

                low_weights(0)
                read_job(before[0])
                low_weights(1)
                read_job(before[1])
                low_weights(2)
                for job in before[2:]:
                    read_job(job)
                for j in range(4):
                    layer_norm_stats(1, j)
                dve.wait_ge(s_const, 4 * 16)
                dve.wait_ge(s_wo_split, 2)
                for t in range(n_quads + 2):
                    first, second, rest = beside[t]
                    if t < n_quads:
                        maxima(2 * t)
                        maxima(2 * t + 1)
                    for job in first:
                        read_job(job)
                    if t < n_quads:
                        inverse_sums(2 * t)
                        inverse_sums(2 * t + 1)
                    for job in second:
                        read_job(job)
                    if t >= 3 and t % 2 == 1:
                        low_outputs((t - 3) // 2)
                    if 1 <= t <= n_quads:
                        copy_transposed(2 * t - 2)
                        copy_transposed(2 * t - 1)
                    for job in rest:
                        read_job(job)
                    if t % 8 >= 4 and t // 8 + 2 < n_batches // 2:
                        layer_norm_stats(t // 8 + 2, t % 4)
                for job in after:
                    read_job(job)

                slots = [1, n_slots, n_experts]
                dve.wait_ge(s_total, 1)
                then_next(dve.tensor_copy(total_e, job_bank(len(all_jobs))[:, 0:n_experts]))
                then_next(dve.tensor_tensor(over, total_e[:, :, None].to_broadcast([P, n_experts, n_over]),
                                            tables[:, None, TAB_BLOCK:TAB_BLOCK + n_over].to_broadcast([P, n_experts, n_over]),
                                            ALU.is_gt))
                then_next(dve.tensor_reduce(blocks_e, over, AXIS_X, ALU.add))
                then_next(dve.tensor_tensor(pre, prefix[:], blocks_e[:, None, :].to_broadcast([P, n_experts, n_experts]), ALU.mult))
                then_next(dve.tensor_reduce(ends, pre, AXIS_X, ALU.add))
                then_next(dve.tensor_tensor(behind, ends[0:1, None, :].to_broadcast(slots),
                                            tables[0:1, TAB_SLOT:TAB_SLOT + n_slots, None].to_broadcast(slots), ALU.is_le))
                then_next(dve.tensor_reduce(slot_e, behind, AXIS_X, ALU.add))
                dve.tensor_copy(slot_i[:, 0, :], slot_e)
                then_next(dve.tensor_scalar(empty_f, ends[0:1, n_experts - 1:n_experts], -1.0, float(n_slots), ALU.mult, ALU.add))
                dve.tensor_copy(empty_i[:], empty_f)
                then_next(dve.tensor_tensor(begun, behind, ends[0:1, None, :].to_broadcast(slots), ALU.mult))
                then_next(dve.tensor_reduce(slot_b, begun, AXIS_X, ALU.max))
                then_next(dve.scalar_tensor_tensor(out=slot_k, in0=slot_b, scalar=-float(BLOCK),
                                                   in1=tables[0:1, TAB_BLOCK:TAB_BLOCK + n_slots], op0=ALU.mult, op1=ALU.add))
                then_next(dve.scalar_tensor_tensor(out=slot_r, in0=slot_e, scalar=float(region), in1=slot_k,
                                                   op0=ALU.mult, op1=ALU.add))
                dve.tensor_copy(slot_i[:, 1, :], slot_r)

            @block.gpsimd
            def _(pool):
                def low_half(b):
                    pool.wait_ge(s_hi, b + 1)
                    pool.tensor_tensor(kv_t[1][:, :, b % 4, :].rearrange("p c (s t) -> p c s t", s=2), y_t[:],
                                       kv_t[0][:, :, b % 4, :].rearrange("p c (s t) -> p c s t", s=2),
                                       ALU.subtract).then_inc(s_lo, 1)

                def soften(n):
                    pool.wait_ge(s_inv, n + 1)
                    probs = prob[:, n % NPROB]
                    pool.tensor_tensor(probs, probs, inv_sum[:, n % 8, :, None].to_broadcast([P, 2, 2 * P]),
                                       ALU.mult).then_inc(s_soft, 1)

                chained = [0]

                def then_next(ins):
                    chained[0] += 1
                    ins.then_inc(s_pool, 1)
                    pool.wait_ge(s_pool, chained[0])

                def inv_sqrt(dst, var):
                    n = var.shape[1]
                    then_next(pool.tensor_scalar(var_eps[:, 0:n], var, EPS, None, ALU.add))
                    return pool.tensor_tensor(dst, var_eps[:, 0:n], minus_half[:, 0:n], ALU.pow)

                def layer_norm_scales(g):
                    pool.wait_ge(s_mv, 4 * (g + 1))
                    if g >= 2:
                        pool.wait_ge(s_nrm, g - 1)
                    scale, shift = ln_scale[:, g % 2, :], ln_shift[:, g % 2, :]
                    mean, var = mean_var[:, :, 0], mean_var[:, :, 1]
                    then_next(inv_sqrt(scale, var))
                    then_next(pool.tensor_tensor(tmp_v[:, 0:2], var[:, 2:4], scale[:, 2:4], ALU.mult))
                    then_next(pool.tensor_tensor(tmp_v[:, 2:4], tmp_v[:, 0:2], scale[:, 2:4], ALU.mult))
                    then_next(inv_sqrt(tmp_v[:, 0:2], tmp_v[:, 2:4]))
                    then_next(pool.tensor_tensor(scale[:, 2:4], scale[:, 2:4], tmp_v[:, 0:2], ALU.mult))
                    then_next(pool.tensor_tensor(shift, mean, scale, ALU.mult))
                    pool.tensor_scalar(shift, shift, -1.0, None, ALU.mult).then_inc(s_lnp, 1)

                def row_scales(b, which, s_from, s_to):
                    pool.wait_ge(s_from, b + 1)
                    col = (COL_S1, COL_S2)[which]
                    row = row_ring[:, b % NROW, :]
                    scale, shift = row[:, col:col + 1], row[:, col + 1:col + 2]
                    then_next(inv_sqrt(scale, mv_z[:, which, 1:2]))
                    then_next(pool.tensor_tensor(shift, mv_z[:, which, 0:1], scale, ALU.mult))
                    pool.tensor_scalar(shift, shift, -1.0, None, ALU.mult).then_inc(s_to, 1)

                then_next(pool.memset(minus_half[:], -0.5))
                def scatter(b):
                    pool.wait_ge(s_pos, b + 1)
                    pool.wait_ge(s_st2, b + 1)
                    if b == n_batches - 2:
                        pool.wait_ge(s_tail, 16 * n_experts)
                    pool.indirect_dma_start(out=sorted_rows, out_offset=bass.IndirectOffsetOnAxis(
                        ap=place_i[:, b % NROW:b % NROW + 1], axis=0),
                        in_=row_ring[:, b % NROW, :], in_offset=None).then_inc(s_scat[b % NROW], 16)

                layer_norm_scales(0)
                pool.memset(filler[:], 0.0).then_inc(s_pad, 1)
                pool.wait_ge(s_pad, 1)
                pool.memset(filler[:].bitcast(I32)[:, COL_TOKEN:COL_TOKEN + 1], OUT_OF_RANGE).then_inc(s_pad, 1)
                low_half(0)
                low_half(1)
                pool.wait_ge(s_wo, 16)
                flat = [w[:].rearrange("p c n -> p (c n)") for w in w_o]
                pool.tensor_copy(flat[0], w_o_raw).then_inc(s_wo_split, 1)
                pool.wait_ge(s_wo_split, 1)
                pool.tensor_tensor(flat[1], w_o_raw, flat[0], ALU.subtract).then_inc(s_wo_split, 1)
                for t in range(n_quads + 2):
                    if t < n_quads:
                        soften(2 * t)
                        soften(2 * t + 1)
                    for job in sum(beside[t], []):
                        if job[0] == "wout":
                            row_scales(job[1], 0, s_mv1, s_st1)
                    for job in sum(beside[t - 1], []) if t else []:
                        if job[0] == "rank":
                            scatter(job[1])
                    for job in sum(beside[t], []):
                        if job[0] == "ln":
                            low_half(job[1])
                        if job[0] == "zt":
                            row_scales(job[1], 1, s_mv2, s_st2)
                    if t == 0:
                        layer_norm_scales(1)
                    elif t % 8 == 7 and t // 8 + 2 < n_batches // 2:
                        layer_norm_scales(t // 8 + 2)
                scatter(n_batches - 2)
                row_scales(n_batches - 1, 0, s_mv1, s_st1)
                row_scales(n_batches - 1, 1, s_mv2, s_st2)
                scatter(n_batches - 1)
                for i in range(NROW):
                    pool.wait_ge(s_scat[i], 16 * len(range(i, n_batches, NROW)))

        with ExitStack() as bb:
            NW = 2
            NR = 4
            width = experts.shape[2]
            n_w = KC * d_ff
            w_ring = [sbuf(bb, f"w{y}_ring", [P, NW, n_w]) for y in (1, 2)]
            vec_ring = sbuf(bb, "vec_ring", [P, NR, width - 2 * n_w])
            b2_ring = sbuf(bb, "b2_ring", [P, NR, d_model])
            w_hl = [[sbuf(bb, f"w{y}_{h}", [P, NW, n_w], F32R) for h in ("hi", "lo")] for y in (1, 2)]
            r_ring = sbuf(bb, "r_ring", [P, NR, 2, ROW])
            zz = sbuf(bb, "zz", [P, 2, 2, d_model])
            xhat = sbuf(bb, "xhat", [P, 2, 2, d_model])
            base = sbuf(bb, "base", [P, NR, 2, d_model])
            xn = sbuf(bb, "xn", [P, KC, BLOCK])
            xn_hl = [sbuf(bb, f"xn_{h}", [P, 2, KC, BLOCK], F32R) for h in ("hi", "lo")]
            hid = sbuf(bb, "hid", [P, FC, BLOCK])
            hid_hl = [sbuf(bb, f"hid_{h}", [P, 2, FC, BLOCK], F32R) for h in ("hi", "lo")]
            upd = sbuf(bb, "upd", [P, 2, d_model])
            fin = sbuf(bb, "fin", [P, 2, 2, d_model])

            f_w = [[sem(f"f_w{y}_{i}") for i in range(NW)] for y in (1, 2)]
            f_v = [sem(f"f_v{i}") for i in range(NR)]
            f_r = [sem(f"f_r{i}") for i in range(NR)]
            f_wh = [sem("f_w1h"), sem("f_w2h")]
            f_wd = [sem("f_w1d"), sem("f_w2d")]
            f_wp = [sem("f_w1p"), sem("f_w2p")]
            f_z = sem("f_z")
            f_xh = sem("f_xh")
            f_base = sem("f_base")
            f_t = sem("f_t")
            f_xa = sem("f_xa")
            f_xd = sem("f_xd")
            f_h = sem("f_h")
            f_ha = sem("f_ha")
            f_hh = sem("f_hh")
            f_hl = sem("f_hl")
            f_y = sem("f_y")
            f_u = sem("f_u")
            f_o = sem("f_o")
            f_out = [sem(f"f_out{i}") for i in range(2)]

            block = bb.enter_context(nc.Block())
            POOL_COLS = 5 * n_w // 16

            n_sure = n_tokens // BLOCK

            def count_empty(eng):
                return eng.value_load(empty_i[0:1, 0:1], min_val=0, max_val=n_slots - n_sure)

            def block_steps(eng, empty):
                def run(s, *steps):
                    if s < n_slots:
                        with eng.If(empty < n_slots - s) if s >= n_sure else nullcontext():
                            for step, *args in steps:
                                step(*args, s)
                return run

            def weights_used(eng, y, s):
                eng.wait_ge(*((f_h, FC // 2 * (s + 1)) if y == 0 else (f_y, 2 * (s + 1))))

            def tr_out(s):
                return psum[:, s % 2, :]

            def hid_out(i):
                return psum[:, 2 + i, :]

            def upd_out(s):
                return psum[:, 6 + s % 2, :]

            @block.sync
            def _(sp):
                def load_weights(y, s):
                    e = expert_of(s)
                    if s >= NW:
                        sp.wait_ge(f_wd[y], s - NW + 1)
                        sp.wait_ge(f_wp[y], s - NW + 1)
                    source = experts[bass.DynSlice(e, 1), :, y * n_w:(y + 1) * n_w].rearrange("o p n -> p (o n)")
                    sp.dma_start(w_ring[y][:, s % NW, :], source).then_inc(f_w[y][s % NW], 16)

                def load_vectors(s):
                    e = expert_of(s)
                    if s >= NR:
                        sp.wait_ge(f_o, 2 * (s - NR) + 2)
                        sp.wait_ge(f_out[(s - NR) % 2], 32 * ((s - NR) // 2 + 1))
                    source = experts[bass.DynSlice(e, 1), :, 2 * n_w:].rearrange("o p n -> p (o n)")
                    sp.dma_start(vec_ring[:, s % NR, :], source).then_inc(f_v[s % NR], 16)
                    sp.dma_start(b2_ring[:, s % NR, :], b2[bass.DynSlice(e, 1), :].to_broadcast([P, d_model])
                                 ).then_inc(f_v[s % NR], 16)

                def load_rows(s):
                    first = sp.value_load(slot_i[0:1, 1, s:s + 1], min_val=0, max_val=n_experts * region - BLOCK)
                    sp.dma_start(r_ring[:, s % NR, :, :], sorted_rows[bass.DynSlice(first, BLOCK), :]
                                 .rearrange("(a p) c -> p a c", p=P)).then_inc(f_r[s % NR], 16)

                def expert_of(s):
                    return sp.value_load(slot_i[0:1, 0, s:s + 1], min_val=0, max_val=n_experts - 1)

                run = block_steps(sp, count_empty(sp))
                load_rows(0)
                load_vectors(0)
                load_weights(0, 0)
                for s in range(1, n_slots + 1):
                    run(s, (load_vectors,), (load_rows,), (load_weights, 0))
                    run(s - 1, (load_weights, 1))

            @block.gpsimd
            def _(pool):
                def low_weights(y, s):
                    pool.wait_ge(f_wh[y], s + 1)
                    if s >= NW:
                        weights_used(pool, y, s - NW)
                    part = slice(0, POOL_COLS)
                    pool.tensor_tensor(w_hl[y][1][:, s % NW, part], w_ring[y][:, s % NW, part], w_hl[y][0][:, s % NW, part],
                                       ALU.subtract).then_inc(f_wp[y], 1)

                def add_base(s):
                    pool.wait_ge(f_z, 2 * s + 2)
                    if s >= NR:
                        pool.wait_ge(f_o, 2 * (s - NR) + 2)
                    pool.tensor_tensor(base[:, s % NR], r_ring[:, s % NR, :, 0:d_model], zz[:, s % 2], ALU.add).then_inc(f_base, 1)

                def write_rows(s):
                    for i in range(2):
                        pool.wait_ge(f_o, 2 * s + i + 1)
                        pool.indirect_dma_start(out=out, out_offset=bass.IndirectOffsetOnAxis(
                            ap=r_ring[:, s % NR, i, COL_TOKEN:COL_TOKEN + 1].bitcast(I32), axis=0),
                            in_=fin[:, s % 2, i, :], in_offset=None,
                            bounds_check=n_tokens - 1, oob_is_err=False).then_inc(f_out[s % 2], 16)

                low_weights(0, 0)
                add_base(0)
                add_base(1)
                low_weights(0, 1)
                low_weights(1, 0)
                empty = count_empty(pool)
                run = block_steps(pool, empty)
                for s in range(n_slots):
                    run(s + 2, (add_base,), (low_weights, 0))
                    run(s + 1, (low_weights, 1))
                    run(s, (write_rows,))
                for s in range(n_sure - 1, n_slots):
                    with pool.If(empty == n_slots - 1 - s):
                        for i in range(2):
                            pool.wait_ge(f_out[(s - i) % 2], 32 * ((s - i) // 2 + 1))

            @block.tensor
            def _(pe):
                def transposes(s):
                    pe.wait_ge(f_xh, s + 1)
                    if s >= 2:
                        pe.wait_ge(f_xa, s - 1)
                    for c in range(KC):
                        for i in range(2):
                            last = pe.transpose(tr_out(s)[:, (2 * c + i) * P:(2 * c + i + 1) * P],
                                                xhat[:, s % 2, i, c * P:(c + 1) * P], ident[:])
                    last.then_inc(f_t, 1)

                def layer_1(s):
                    pe.wait_ge(f_xd, 2 * s + 2)
                    pe.wait_ge(f_wd[0], s + 1)
                    pe.wait_ge(f_wp[0], s + 1)
                    for f in range(FC):
                        if f % 2 == 0 and s >= 1:
                            pe.wait_ge(f_ha, FC * (s - 1) + f + 2)
                        dst = hid_out(f // 2)[:, (f % 2) * BLOCK:(f % 2 + 1) * BLOCK]
                        for i, (hw, hx) in enumerate(PASSES):
                            w1 = w_hl[0][hw][:, s % NW, :].rearrange("p (c f) -> p c f", c=KC)
                            for c in range(KC):
                                last = pe.matmul(dst, w1[:, c, f * P:(f + 1) * P], xn_hl[hx][:, s % 2, c, :],
                                                 start=(i == 0 and c == 0), stop=(i == 2 and c == KC - 1))
                        if f % 2 == 1:
                            last.then_inc(f_h, 1)

                def layer_2(s):
                    pe.wait_ge(f_wd[1], s + 1)
                    pe.wait_ge(f_wp[1], s + 1)
                    if s >= 2:
                        pe.wait_ge(f_u, 2 * (s - 2) + 2)
                    for i in range(2):
                        dst = upd_out(s)[:, i * d_model:(i + 1) * d_model]
                        for f in range(FC):
                            if f % 4 == 0 and i == 0:
                                pe.wait_ge(f_hl, 2 * s + f // 4 + 1)
                            for j, (hh, hw) in enumerate(PASSES):
                                w2 = w_hl[1][hw][:, s % NW, :].rearrange("p (f d) -> p f d", f=FC)
                                last = pe.matmul(dst, hid_hl[hh][:, s % 2, f, i * P:(i + 1) * P], w2[:, f, :],
                                                 start=(f == 0 and j == 0), stop=(f == FC - 1 and j == 2))
                        last.then_inc(f_y, 1)

                transposes(0)
                transposes(1)
                layer_1(0)
                run = block_steps(pe, count_empty(pe))
                for s in range(n_slots):
                    run(s + 1, (layer_1,))
                    run(s + 2, (transposes,))
                    run(s, (layer_2,))

            @block.scalar
            def _(act):
                def high_weights(y, s):
                    act.wait_ge(f_w[y][s % NW], 16 * (s // NW + 1))
                    if s >= NW:
                        weights_used(act, y, s - NW)
                    act.activation(w_hl[y][0][:, s % NW, :], w_ring[y][:, s % NW, :], ACT.Copy).then_inc(f_wh[y], 1)

                def z_of(s):
                    act.wait_ge(f_r[s % NR], 16 * (s // NR + 1))
                    if s >= 2:
                        act.wait_ge(f_xh, s - 1)
                        act.wait_ge(f_base, s - 1)
                    for i in range(2):
                        row = r_ring[:, s % NR, i, :]
                        act.activation(zz[:, s % 2, i, :], row[:, 0:d_model], ACT.Identity, bias=row[:, COL_T1:COL_T1 + 1],
                                       scale=row[:, COL_S1:COL_S1 + 1]).then_inc(f_z, 1)

                def gain_bias(s):
                    act.wait_ge(f_t, s + 1)
                    act.wait_ge(f_v[s % NR], 32 * (s // NR + 1))
                    if s >= 1:
                        act.wait_ge(f_xd, 2 * s)
                    vec = vec_ring[:, s % NR, 0:2 * KC]
                    for c in range(KC):
                        last = act.activation(xn[:, c, :], tr_out(s)[:, c * BLOCK:(c + 1) * BLOCK], ACT.Identity,
                                              bias=vec[:, KC + c:KC + c + 1], scale=vec[:, c:c + 1])
                    last.then_inc(f_xa, 1)

                def relu(s):
                    b1 = vec_ring[:, s % NR, 2 * KC:]
                    for f in range(FC):
                        if f % 2 == 0:
                            act.wait_ge(f_h, FC // 2 * s + f // 2 + 1)
                        if s >= 1 and f % 4 == 0:
                            act.wait_ge(f_hl, 2 * (s - 1) + f // 4 + 1)
                        act.activation(hid[:, f, :], hid_out(f // 2)[:, (f % 2) * BLOCK:(f % 2 + 1) * BLOCK], ACT.Relu,
                                       bias=b1[:, f:f + 1]).then_inc(f_ha, 1)

                z_of(0)
                gain_bias(0)
                high_weights(0, 0)
                z_of(1)
                gain_bias(1)
                high_weights(0, 1)
                relu(0)
                high_weights(1, 0)
                run = block_steps(act, count_empty(act))
                for s in range(n_slots):
                    run(s + 2, (z_of,), (high_weights, 0))
                    run(s + 1, (relu,))
                    run(s + 2, (gain_bias,))
                    run(s + 1, (high_weights, 1))

            @block.vector
            def _(dve):
                def prepare(s):
                    if s >= 2:
                        dve.wait_ge(f_t, s - 1)
                    for i in range(2):
                        row = r_ring[:, s % NR, i, :]
                        dve.wait_ge(f_z, 2 * s + i + 1)
                        ins = dve.tensor_scalar(xhat[:, s % 2, i, :], zz[:, s % 2, i, :], row[:, COL_S2:COL_S2 + 1],
                                                row[:, COL_T2:COL_T2 + 1], ALU.mult, ALU.add)
                    ins.then_inc(f_xh, 1)

                def split_xn(s):
                    dve.wait_ge(f_xa, s + 1)
                    if s >= 2:
                        dve.wait_ge(f_h, FC // 2 * (s - 1))
                    dve.tensor_copy(xn_hl[0][:, s % 2], xn[:]).then_inc(f_xd, 1)
                    dve.wait_ge(f_xd, 2 * s + 1)
                    dve.tensor_tensor(xn_hl[1][:, s % 2], xn[:], xn_hl[0][:, s % 2], ALU.subtract).then_inc(f_xd, 1)

                def low_weights(y, s):
                    dve.wait_ge(f_wh[y], s + 1)
                    if s >= NW:
                        weights_used(dve, y, s - NW)
                    part = slice(POOL_COLS, n_w)
                    dve.tensor_tensor(w_hl[y][1][:, s % NW, part], w_ring[y][:, s % NW, part], w_hl[y][0][:, s % NW, part],
                                      ALU.subtract).then_inc(f_wd[y], 1)

                def split_hid(s):
                    for half in range(2):
                        part = slice(half * FC // 2, (half + 1) * FC // 2)
                        dve.wait_ge(f_ha, FC * s + (half + 1) * FC // 2)
                        if s >= 2 and half == 0:
                            dve.wait_ge(f_y, 2 * s - 2)
                        dve.tensor_copy(hid_hl[0][:, s % 2, part, :], hid[:, part, :]).then_inc(f_hh, 1)
                        dve.wait_ge(f_hh, 2 * s + half + 1)
                        dve.tensor_tensor(hid_hl[1][:, s % 2, part, :], hid[:, part, :], hid_hl[0][:, s % 2, part, :], ALU.subtract).then_inc(f_hl, 1)

                def finish(s):
                    dve.wait_ge(f_y, 2 * s + 2)
                    dve.wait_ge(f_o, 2 * s)
                    for i in range(2):
                        dve.tensor_tensor(upd[:, i, :], upd_out(s)[:, i * d_model:(i + 1) * d_model], b2_ring[:, s % NR, :],
                                          ALU.add).then_inc(f_u, 1)
                    dve.wait_ge(f_base, s + 1)
                    if s >= 2:
                        dve.wait_ge(f_out[s % 2], 32 * (s // 2))
                    for i in range(2):
                        dve.wait_ge(f_u, 2 * s + i + 1)
                        dve.scalar_tensor_tensor(out=fin[:, s % 2, i, :], in0=upd[:, i, :],
                                                 scalar=r_ring[:, s % NR, i, COL_ALPHA:COL_ALPHA + 1],
                                                 in1=base[:, s % NR, i, :], op0=ALU.mult, op1=ALU.add).then_inc(f_o, 1)

                prepare(0)
                split_xn(0)
                low_weights(0, 0)
                prepare(1)
                split_xn(1)
                low_weights(0, 1)
                split_hid(0)
                low_weights(1, 0)
                run = block_steps(dve, count_empty(dve))
                for s in range(n_slots):
                    run(s + 2, (prepare,), (low_weights, 0))
                    run(s + 1, (split_hid,))
                    run(s + 2, (split_xn,))
                    run(s + 1, (low_weights, 1))
                    run(s, (finish,))


def kernel(x, ctx_1024, L0_xattn_ln_m_g, L0_xattn_ln_m_b, L0_xattn_ln_l_g, L0_xattn_ln_l_b, L0_xattn_Wq, L0_xattn_Wkv,
           L0_xattn_Wout, L0_ffn_centroids, L0_ffn_ln_g, L0_ffn_ln_b, L0_ffn_w1, L0_ffn_b1, L0_ffn_w2, L0_ffn_b2):
    import numpy as np
    import concourse.bacc as bacc
    from concourse.bass_utils import run_bass_kernel_spmd

    p = 128
    n_batches, n_tok, d_model = x.shape
    n_experts, d_ff, _ = L0_ffn_w1.shape
    kc, fc = d_model // p, d_ff // p
    n_tokens = n_batches * n_tok
    n_slots = n_tokens // BLOCK + n_experts - 1

    def columns(v):
        v = np.asarray(v)
        return np.swapaxes(v.reshape(*v.shape[:-1], -1, p), -1, -2)

    ln_pack = np.stack([columns(v) for v in (L0_xattn_ln_m_g, L0_xattn_ln_m_b, L0_xattn_ln_l_g, L0_xattn_ln_l_b)], axis=1)
    centroids_t = np.asarray(L0_ffn_centroids).T.reshape(kc, p, n_experts).transpose(1, 0, 2)
    w1 = np.asarray(L0_ffn_w1).transpose(0, 2, 1).reshape(n_experts, kc, p, d_ff).transpose(0, 2, 1, 3)
    w2 = np.asarray(L0_ffn_w2).transpose(0, 2, 1).reshape(n_experts, fc, p, d_model).transpose(0, 2, 1, 3)
    experts = np.concatenate([w1.reshape(n_experts, p, -1), w2.reshape(n_experts, p, -1),
                              columns(L0_ffn_ln_g), columns(L0_ffn_ln_b), columns(L0_ffn_b1)], axis=2)

    consts = np.zeros((p, 3 * p + N_TABLE + n_experts ** 2), np.float32)
    consts[:, 0:p] = np.eye(p)
    consts[:, p:2 * p] = np.triu(np.ones((p, p)), 1)
    consts[:, 2 * p:3 * p] = 1.0
    tables = consts[:, 3 * p:3 * p + N_TABLE]
    tables[:, TAB_RANK:TAB_RANK + n_experts] = n_experts - np.arange(n_experts)
    tables[:, TAB_REGION:TAB_REGION + n_experts] = (n_tokens + BLOCK) * np.arange(n_experts)
    tables[:, TAB_BLOCK:TAB_BLOCK + n_slots] = BLOCK * np.arange(n_slots)
    tables[:, TAB_SLOT:TAB_SLOT + n_slots] = np.arange(n_slots)
    tables[:, TAB_TOKEN:TAB_TOKEN + n_batches] = np.arange(n_batches)[None, :] * p + np.arange(p)[:, None]
    consts[:, 3 * p + N_TABLE:] = np.tril(np.ones((n_experts, n_experts))).reshape(-1)

    arrays = {"x": x, "ctx_in": ctx_1024, "ln_pack": ln_pack, "w_q": L0_xattn_Wq, "w_kv": L0_xattn_Wkv,
              "w_out": L0_xattn_Wout, "centroids_t": centroids_t, "consts": consts, "experts": experts, "b2": L0_ffn_b2}
    arrays = {f"in_{k}": np.ascontiguousarray(v) for k, v in arrays.items()}
    nc = bacc.Bacc("TRN2", target_bir_lowering=False, num_devices=1)
    args = [nc.dram_tensor(k, v.shape, mybir.dt.from_np(v.dtype), kind="ExternalInput").ap() for k, v in arrays.items()]
    out = nc.dram_tensor("out", (n_batches * n_tok, d_model), F32, kind="ExternalOutput").ap()
    build(nc, *args, out)
    r = run_bass_kernel_spmd(nc, [arrays], core_ids=[0])
    return r.results[0]["out"].reshape(n_batches, n_tok, d_model)
```
